# Optimizing a Trainium2 kernel written in Bass

```python
import numpy as np
import jax
import jax.numpy as jnp

def _softmax(x, axis=-1):
    return jax.nn.softmax(x, axis=axis)

def _gelu(x):
    return jax.nn.gelu(x, approximate=True)

def _silu(x):
    return jax.nn.silu(x)

def _sigmoid(x):
    return jax.nn.sigmoid(x)

def _layernorm(x, axis=-1, eps=1e-05):
    m = jnp.mean(x, axis=axis, keepdims=True)
    v = jnp.var(x, axis=axis, keepdims=True)
    return (x - m) / jnp.sqrt(v + eps)

def _scatter_add(tgt, idx, src, axis=0):
    return tgt.at[idx].add(src)

def _segment_sum(src, seg, n):
    return jax.ops.segment_sum(src, seg, n)
kernel_name = 'mk_xattn_ffn_d1_seqx_r4_6bf2ae'

def setup_inputs(seed: int=0):
    np.random.seed(seed)
    _w = jnp.asarray

    def _rec_inputs():
        import jax
        import jax.numpy as jnp
        _rk = jax.random.key(seed)
        x = 7.22e-05 + 1 * jax.random.normal(jax.random.fold_in(_rk, 1), (32, 256, 256), jnp.float32)
        _lenS = 256 - jax.random.randint(jax.random.fold_in(_rk, 7), (32,), 0, max(1, 256 // 4) + 1, jnp.int32)
        _lenS2 = 256 - jax.random.randint(jax.random.fold_in(_rk, 8), (32,), 0, max(1, 256 // 4) + 1, jnp.int32)
        fside_BxSxS_0 = 4.13588e-05 + 0.999923 * jax.random.normal(jax.random.fold_in(_rk, 11), (32, 256, 256), jnp.float32)
        _ctx_1024P = jax.random.normal(jax.random.fold_in(_rk, 13), (32, 16, 256), jnp.float32)
        _ctx_1024c = jax.random.dirichlet(jax.random.fold_in(_rk, 513), 0.3 * jnp.ones((16,), jnp.float32), (32, 256))
        _ctx_1024t = jnp.einsum('bsk,bkd->bsd', _ctx_1024c, _ctx_1024P)
        _ctx_1024t = _ctx_1024t * jax.lax.rsqrt(jnp.mean(jnp.square(_ctx_1024t)) + 1e-12) * 0.953939
        ctx_1024 = 0.00513834 + 0.998274 * (_ctx_1024t + 0.3 * jax.random.normal(jax.random.fold_in(_rk, 613), (32, 256, 256), jnp.float32))
        _validS = jnp.arange(256)[None, :] < _lenS[:, None]
        _validS2 = jnp.arange(256)[None, :] < _lenS2[:, None]
        _causal = jnp.tril(jnp.ones((256, 256), dtype=bool))
        mask_Bx16xSxS_bk1 = jnp.broadcast_to(_validS[:, None, None, :], (32, 16, 256, 256))
        return (x, fside_BxSxS_0, ctx_1024, mask_Bx16xSxS_bk1)
    x, fside_BxSxS_0, ctx_1024, mask_Bx16xSxS_bk1 = _rec_inputs()

    def _L0_xattn_setup():
        import jax, jax.numpy as jnp
        import numpy as np
        D_MODEL, D_K, D_V, H = (256, 64, 64, 16)
        B, NQ, NK, M = (8, 256, 256, 49)

        def _xavier(key, shape):
            fan_in, fan_out = (shape[1], shape[0])
            limit = float(np.sqrt(6.0 / (fan_in + fan_out)))
            return jax.random.uniform(key, shape, jnp.float32, -limit, limit)
        key = jax.random.key(seed)
        ks = jax.random.split(key, 12)
        inp = {'queries': jax.random.normal(ks[0], (B, NQ, D_MODEL), jnp.float32), 'keys': jax.random.normal(ks[1], (B, NK, D_MODEL), jnp.float32), 'values': jax.random.normal(ks[2], (B, NK, D_MODEL), jnp.float32), 'attention_mask': jax.random.randint(ks[3], (B, H, NQ, NK), 0, 2) > 0, 'key_grid': jax.random.normal(ks[4], (B, M, D_MODEL), jnp.float32), 'value_grid': jax.random.normal(ks[5], (B, M, D_MODEL), jnp.float32), 'Wq': _xavier(ks[6], (H * D_K, D_MODEL)), 'bq': jnp.zeros((H * D_K,), jnp.float32), 'Wk': _xavier(ks[7], (H * D_K, D_MODEL)), 'bk': jnp.zeros((H * D_K,), jnp.float32), 'Wgk': _xavier(ks[8], (H * D_K, D_MODEL)), 'bgk': jnp.zeros((H * D_K,), jnp.float32), 'Wv': _xavier(ks[9], (H * D_V, D_MODEL)), 'bv': jnp.zeros((H * D_V,), jnp.float32), 'Wgv': _xavier(ks[10], (H * D_V, D_MODEL)), 'bgv': jnp.zeros((H * D_V,), jnp.float32), 'Wo': _xavier(ks[11], (D_MODEL, H * D_V)), 'bo': jnp.zeros((D_MODEL,), jnp.float32)}
        return inp
    _L0_xattn_all = _L0_xattn_setup()
    _L0_xattn_in = {k: v for k, v in _L0_xattn_all.items() if k in ('Wq', 'bq', 'Wk', 'bk', 'Wgk', 'bgk', 'Wv', 'bv', 'Wgv', 'bgv', 'Wo', 'bo')}
    del _L0_xattn_all

    def _L0_ffn_setup():
        import jax, jax.numpy as jnp
        import numpy as np
        FEATURES = 256
        D_IN = 256

        def fp8_gemm_optimized(x, input_scale, kernel, kernel_scale):
            s_in = input_scale[0]
            s_k = kernel_scale[0]
            x_q = (x.astype(jnp.float32) / s_in).astype(jnp.float8_e4m3fn)
            k_q = (kernel.astype(jnp.float32) / s_k).astype(jnp.float8_e4m3fn)
            y = jnp.dot(x_q.astype(jnp.float32), k_q.astype(jnp.float32), preferred_element_type=jnp.float32)
            return y * (s_in * s_k)
        key = jax.random.key(seed)
        kx, kk, kb = jax.random.split(key, 3)
        x = jax.random.normal(kx, (4, 2048, D_IN), dtype=jnp.float32)
        limit = np.sqrt(6.0 / (D_IN + FEATURES)).astype(np.float32)
        kernel = jax.random.uniform(kk, (D_IN, FEATURES), dtype=jnp.float32, minval=-limit, maxval=limit).astype(jnp.bfloat16)
        input_scale = jnp.ones((1,), dtype=jnp.float32)
        kernel_scale = jnp.ones((1,), dtype=jnp.float32)
        bias = jnp.zeros((FEATURES,), dtype=jnp.bfloat16)
        return {'x': x, 'kernel': kernel, 'input_scale': input_scale, 'kernel_scale': kernel_scale, 'bias': bias}
    _L0_ffn_all = _L0_ffn_setup()
    _L0_ffn_in = {k: v for k, v in _L0_ffn_all.items() if k in ('kernel', 'input_scale', 'kernel_scale', 'bias')}
    del _L0_ffn_all
    return {'x': x, 'fside_BxSxS_0': fside_BxSxS_0, 'ctx_1024': ctx_1024, 'mask_Bx16xSxS_bk1': mask_Bx16xSxS_bk1, 'L0_xattn_Wq': _L0_xattn_in['Wq'], 'L0_xattn_bq': _L0_xattn_in['bq'], 'L0_xattn_Wk': _L0_xattn_in['Wk'], 'L0_xattn_bk': _L0_xattn_in['bk'], 'L0_xattn_Wgk': _L0_xattn_in['Wgk'], 'L0_xattn_bgk': _L0_xattn_in['bgk'], 'L0_xattn_Wv': _L0_xattn_in['Wv'], 'L0_xattn_bv': _L0_xattn_in['bv'], 'L0_xattn_Wgv': _L0_xattn_in['Wgv'], 'L0_xattn_bgv': _L0_xattn_in['bgv'], 'L0_xattn_Wo': _L0_xattn_in['Wo'], 'L0_xattn_bo': _L0_xattn_in['bo'], 'L0_ffn_kernel': _L0_ffn_in['kernel'], 'L0_ffn_input_scale': _L0_ffn_in['input_scale'], 'L0_ffn_kernel_scale': _L0_ffn_in['kernel_scale'], 'L0_ffn_bias': _L0_ffn_in['bias']}

def reference(x, fside_BxSxS_0, ctx_1024, mask_Bx16xSxS_bk1, L0_xattn_Wq, L0_xattn_bq, L0_xattn_Wk, L0_xattn_bk, L0_xattn_Wgk, L0_xattn_bgk, L0_xattn_Wv, L0_xattn_bv, L0_xattn_Wgv, L0_xattn_bgv, L0_xattn_Wo, L0_xattn_bo, L0_ffn_kernel, L0_ffn_input_scale, L0_ffn_kernel_scale, L0_ffn_bias):
    import jax
    import jax.numpy as jnp

    def _L0_xattn_ref(queries, keys, values, attention_mask, key_grid, value_grid, Wq, bq, Wk, bk, Wgk, bgk, Wv, bv, Wgv, bgv, Wo, bo):
        import jax, jax.numpy as jnp
        import numpy as np
        D_MODEL, D_K, D_V, H = (256, 64, 64, 16)
        B, NQ, NK, M = (8, 256, 256, 49)

        def _xavier(key, shape):
            fan_in, fan_out = (shape[1], shape[0])
            limit = float(np.sqrt(6.0 / (fan_in + fan_out)))
            return jax.random.uniform(key, shape, jnp.float32, -limit, limit)
        b_s, nq, _ = queries.shape
        nk = keys.shape[1]
        scale = 1.0 / np.sqrt(D_K)
        k = keys @ Wk.T + bk
        gk = key_grid @ Wgk.T + bgk
        k_new = jnp.concatenate([k, gk], axis=1)
        k_new = k_new.reshape(b_s, -1, H, D_K).transpose(0, 2, 3, 1)
        v = values @ Wv.T + bv
        gv = key_grid @ Wgv.T + bgv
        v_new = jnp.concatenate([v, gv], axis=1)
        v_new = v_new.reshape(b_s, -1, H, D_V).transpose(0, 2, 1, 3)
        q = (queries @ Wq.T + bq).reshape(b_s, nq, H, D_K).transpose(0, 2, 1, 3)
        att = jnp.einsum('bhqd,bhdk->bhqk', q, k_new) * scale
        att_k = jnp.where(attention_mask, -jnp.inf, att[..., :nk])
        att = jnp.concatenate([att_k, att[..., nk:]], axis=-1)
        att = jax.nn.softmax(att, axis=-1)
        out = jnp.einsum('bhqk,bhkd->bhqd', att, v_new)
        out = out.transpose(0, 2, 1, 3).reshape(b_s, nq, H * D_V)
        return out @ Wo.T + bo

    def _L0_ffn_ref(x, kernel, input_scale, kernel_scale, bias):
        import jax, jax.numpy as jnp
        import numpy as np
        FEATURES = 256
        D_IN = 256

        def fp8_gemm_optimized(x, input_scale, kernel, kernel_scale):
            s_in = input_scale[0]
            s_k = kernel_scale[0]
            x_q = (x.astype(jnp.float32) / s_in).astype(jnp.float8_e4m3fn)
            k_q = (kernel.astype(jnp.float32) / s_k).astype(jnp.float8_e4m3fn)
            y = jnp.dot(x_q.astype(jnp.float32), k_q.astype(jnp.float32), preferred_element_type=jnp.float32)
            return y * (s_in * s_k)
        dtype = jnp.bfloat16
        x = x.astype(dtype)
        orig_shape = x.shape
        x2 = x.reshape(-1, x.shape[-1])
        y = fp8_gemm_optimized(x2, input_scale, kernel, kernel_scale)
        y = y.astype(dtype) + bias
        return y.reshape(orig_shape[:-1] + (FEATURES,))
    x = x + _L0_xattn_ref(_layernorm(x, axis=-1), fside_BxSxS_0, fside_BxSxS_0, mask_Bx16xSxS_bk1, ctx_1024, ctx_1024, L0_xattn_Wq, L0_xattn_bq, L0_xattn_Wk, L0_xattn_bk, L0_xattn_Wgk, L0_xattn_bgk, L0_xattn_Wv, L0_xattn_bv, L0_xattn_Wgv, L0_xattn_bgv, L0_xattn_Wo, L0_xattn_bo)
    x = x + _L0_ffn_ref(_layernorm(x, axis=-1), L0_ffn_kernel, L0_ffn_input_scale, L0_ffn_kernel_scale, L0_ffn_bias)
    return x

_drawn_inputs = setup_inputs


def setup_inputs(seed=0):
    import zlib

    import numpy as np

    out = dict(_drawn_inputs(seed))
    spreads = {'L0_xattn_bq': (0.0, 0.476),
     'L0_xattn_bk': (0.0, 0.8),
     'L0_xattn_bgk': (0.0, 0.8),
     'L0_xattn_bv': (0.0, 0.4),
     'L0_xattn_bgv': (0.0, 0.8),
     'L0_xattn_bo': (0.0, 0.415),
     'L0_ffn_bias': (0.0, 0.412)}
    factors = {'fside_BxSxS_0': 2.845, 'L0_xattn_Wk': 4.757, 'L0_xattn_Wv': 2.862, 'L0_xattn_Wgk': 3.139}
    for name, (base, spread) in spreads.items():
        noise = np.random.default_rng([zlib.crc32(name.encode()), seed]).standard_normal(out[name].shape)
        drawn = base * np.exp(spread * noise) if base else spread * noise
        out[name] = jnp.asarray(drawn.astype(out[name].dtype))
    for name, factor in factors.items():
        out[name] = (out[name] * factor).astype(out[name].dtype)
    return out
```

```python
from contextlib import ExitStack

import concourse.bass as bass
from concourse import mybir

F32 = mybir.dt.float32
F32R = mybir.dt.float32r
BF16 = mybir.dt.bfloat16
FP8E5 = mybir.dt.float8e5
U8 = mybir.dt.uint8
U32 = mybir.dt.uint32
ALU = mybir.AluOpType
ACT = mybir.ActivationFunctionType
AX_X = mybir.AxisListType.X

P = 128
B, S, D, H = 32, 256, 256, 16
DK = 64
NK = 2 * S
QT = S // P
DT = D // P
KT = NK // P
GH = 4
NG = H // GH
GW = GH * DK
SCORE_SCALE = -1.0 / DK ** 0.5
LN_EPS = 1e-5
MASK_WEIGHT = 2.0 ** 116
E4_MAGIC = 1.5 * 2.0 ** 20
E4_MIN_NORMAL = 2.0 ** -6
E4_OVERFLOW = 1.69e33

PLACES = {
    (1, "A"): ("wo_prev", 0), (5, "C"): ("xq_prev", 0), (7, "A"): ("ff_prev", 0), (11, "A"): ("zt_next", 0),
    (0, "A"): ("q", 1), (0, "B"): ("k0", 1), (1, "B"): ("k1", 1), (2, "A"): ("v0", 1), (2, "B"): ("v1", 1),
    (4, "A"): ("q", 2), (4, "B"): ("k0", 2), (5, "A"): ("k1", 2), (5, "B"): ("v0", 2), (6, "A"): ("v1", 2),
    (8, "A"): ("q", 3), (8, "B"): ("k0", 3), (9, "A"): ("k1", 3), (9, "B"): ("v0", 3), (10, "A"): ("v1", 3),
    (12, "A"): ("q", 0), (12, "B"): ("k0", 0), (13, "A"): ("k1", 0), (13, "B"): ("v0", 0), (14, "A"): ("v1", 0),
}
SLOT_ORDER = [(h, place) for h in range(H) for place in "ABC"]
PROLOGUE = [("zt_next", 0), ("q", 0), ("k0", 0), ("k1", 0), ("v0", 0), ("v1", 0)]
PREV = ("wo_prev", "xq_prev", "ff_prev")


def chunks_of(first, last):
    def kept(place, chunk):
        kind, group = chunk
        if first and kind in PREV:
            return False
        return not (last and (kind == "zt_next" or place[0] >= 12))
    return {place: PLACES[place] for place in SLOT_ORDER if place in PLACES and kept(place, PLACES[place])}


FIRST = list(chunks_of(True, False).values())
STEADY = list(chunks_of(False, False).values())
SPLIT = ("zt_next", "q", "k0", "k1", "v0", "v1")


def count_before(b, kinds):
    per = sum(kind in kinds for kind, _ in STEADY)
    head = sum(kind in kinds for kind, _ in PROLOGUE)
    if isinstance(b, int) and b == 0:
        return head
    return per * b + (head + sum(kind in kinds for kind, _ in FIRST) - per)


ALL_KINDS = SPLIT + PREV


TAIL_AT = count_before(B - 1, ALL_KINDS) + len(chunks_of(False, True))
TOTAL_CHUNKS = TAIL_AT + len(PREV)


class Chunks:

    def __init__(self, b, first=False, last=False):
        self.b, self.at = b, chunks_of(first, last)
        self.order = list(self.at)

    def before(self, place, kinds=ALL_KINDS):
        n = sum(self.at[p][0] in kinds for p in self.order[:self.order.index(place)])
        return count_before(self.b, kinds) + n

    def through(self, kind, group):
        for p in self.order:
            if self.at[p] == (kind, group):
                return self.before(p) + 1
        raise KeyError(kind)


def xattn_ffn_kernel(nc, x, side_t, ctx_t, mask, wq_t, bq, wk_t, bk, wgk_t, bgk, wv_t, bv, wgv_t, bgv,
                     wo_t, bo, ffn_w, s_in, s_k, ffn_bias, out):
    with ExitStack() as ctx:
        def sb(name, shape, dt):
            return ctx.enter_context(nc.sbuf_tensor(name, shape, dt))

        def psum(name, shape, dt=F32):
            return ctx.enter_context(nc.psum_tensor(name, shape, dt))

        def sem(name):
            return ctx.enter_context(nc.semaphore(name))

        names = ["q", "k", "gk", "v", "gv"]
        w_hi = {n: sb(f"w{n}_hi", [P, DT, H * DK], F32R) for n in names}
        w_lo = {n: sb(f"w{n}_lo", [P, DT, H * DK], F32R) for n in names}
        wo_sb = sb("wo_sb", [P, H * DK // P, D], F32)
        ffn_q = sb("ffn_q", [P, DT, D], BF16)
        vbias = sb("vbias", [P, 2, H * DK], BF16)
        vbias_ones = sb("vbias_ones", [P, P], BF16)
        qk_bias = sb("qk_bias", [P, 3, H * DK // P], F32)
        bo_rows = sb("bo_rows", [P, D], F32)
        fb_rows = sb("fb_rows", [P, D], BF16)
        scales = sb("scales", [P, 8], F32)
        ident = sb("ident", [P, P], F32)
        ident_bf = sb("ident_bf", [P, P], BF16)
        mask_weight = sb("mask_weight", [P, P], BF16)

        side_raw = sb("side_raw", [P, DT, S], F32)
        kv_hi = sb("kv_hi", [P, DT, NK], F32R)
        kv_lo = sb("kv_lo", [P, DT, NK], F32R)
        x_sb = sb("x_sb", [P, QT, D], F32)
        xbo = sb("xbo", [P, QT, D], F32)
        zt_hi = sb("zt_hi", [P, DT, S], F32R)
        zt_lo = sb("zt_lo", [P, DT, S], F32R)
        o_t = sb("o_t", [P, H // 2, S], F32)
        y = sb("y", [P, QT, D], F32)
        scr_a = sb("scr_a", [P, QT * D], F32)
        scr_b = sb("scr_b", [P, QT * D], F32)
        z2 = sb("z2", [P, QT * D], BF16)
        xq = sb("xq", [P, QT * D], BF16)
        xq_t = z2[:].rearrange("p (t s) -> p t s", t=DT)
        f1 = xq[:].rearrange("p (t d) -> p t d", t=QT)
        stats = sb("stats", [P, 2, QT, 6], F32)
        mv = sb("mv", [P, 2, QT, 2], F32)
        var_eps = sb("var_eps", [P, 2, QT], F32)
        rstd = sb("rstd", [P, 2, QT], F32)
        minus_half = sb("minus_half", [P, QT], F32)

        q_hi = sb("q_hi", [P, 2, GH, S], F32R)
        q_lo = sb("q_lo", [P, 2, GH, S], F32R)
        k_hi = sb("k_hi", [P, 2, GH // 2, NK], F32R)
        k_lo = sb("k_lo", [P, 2, GH // 2, NK], F32R)
        v_hl = sb("v_hl", [P, 2, KT, GH, 2 * DK], F32R)
        mask_sb = sb("mask_sb", [P, 2, GH * QT * S], U8)
        probs = sb("probs", [P, 2, QT, NK], F32)
        pt_hi = sb("pt_hi", [P, 2, KT, S], F32R)
        pt_lo = sb("pt_lo", [P, 2, KT, S], F32R)
        neg_max = sb("neg_max", [P, 2, QT], F32)
        sums = sb("sums", [P, 2, QT], F32)
        recips = sb("recips", [P, 2, QT], F32)
        o_lo = sb("o_lo", [DK, S], F32)

        ps_scores = psum("ps_scores", [P, 2, QT, NK])
        ps_pt = psum("ps_pt", [P, 2, 2, S])
        ps_o = psum("ps_o", [P, 512])
        ps_misc = psum("ps_misc", [P, 512])

        w_loaded = [sem("w_loaded0"), sem("w_loaded1")]
        w_split = sem("w_split")
        w_hi_done = sem("w_hi_done")
        consts_loaded = sem("consts_loaded")
        wo_loaded = sem("wo_loaded")
        ident_zero = sem("ident_zero")
        ident_done = sem("ident_done")
        consts_done = sem("consts_done")
        ffn_chain = sem("ffn_chain")
        prep_chain = sem("prep_chain")
        zeros_done = sem("zeros_done")
        mask_loaded = [sem("mask_loaded0"), sem("mask_loaded1")]
        side_loaded = sem("side_loaded")
        ctx_loaded = sem("ctx_loaded")
        x_loaded = sem("x_loaded")
        out_stored = sem("out_stored")
        scores_done = sem("scores_done")
        pt_full = sem("pt_full")
        o_full = sem("o_full")
        misc_full = sem("misc_full")
        misc_free = sem("misc_free")
        hi_done = sem("hi_done")
        exp_done = sem("exp_done")
        pthi_done = sem("pthi_done")
        ptlo_done = sem("ptlo_done")
        olo_done = sem("olo_done")
        o_done = sem("o_done")
        min_done = sem("min_done")
        recip_done = sem("recip_done")
        norm_done = sem("norm_done")
        kvhi_done = sem("kvhi_done")
        kv_split = sem("kv_split")
        xbo_done = sem("xbo_done")
        bn_x = sem("bn_x")
        mv_x = sem("mv_x")
        var_x = sem("var_x")
        rstd_x = sem("rstd_x")
        z_done = sem("z_done")
        bn_y = sem("bn_y")
        mv_y = sem("mv_y")
        var_y = sem("var_y")
        rstd_y = sem("rstd_y")
        z2_done = sem("z2_done")
        v_done = sem("v_done")
        quant_chain = sem("quant_chain")
        xq_done = sem("xq_done")
        f2_done = sem("f2_done")
        out_done = sem("out_done")

        QUANT_STEPS = 5
        w_src = {"q": wq_t, "k": wk_t, "gk": wgk_t, "v": wv_t, "gv": wgv_t}
        stage = [probs[:].rearrange("p a b c -> p (a b c)"), o_t[:].rearrange("p a b -> p (a b)")]
        s_in_col, s_k_col, rs_in_col, rs_k_col, ss_col = (scales[:, i:i + 1] for i in range(5))

        block = ctx.enter_context(nc.Block())

        waits_passed = {e: sem(f"waits_passed_{e}") for e in ("sp", "pool", "dve")}

        def wait_apart(engine, name, semaphore, value):
            engine.wait_ge(semaphore, value)
            engine.sem_inc(waits_passed[name], 1)

        @block.sync
        def _(sp):
            def load_mask(b, n):
                if not (isinstance(b, int) and b == 0 and n < 2):
                    wait_apart(sp, "sp", scores_done, H * b + GH * (n - 1))
                src = one(mask, b).rearrange("o p n -> (o p) n")
                sp.dma_start(mask_sb[:, n % 2, :],
                             src[:, n * GH * QT * S:(n + 1) * GH * QT * S]).then_inc(mask_loaded[n % 2], 16)

            def one(ap, b):
                return ap[b:b + 1] if isinstance(b, int) else ap[bass.ds(b, 1)]

            def load_x(b):
                sp.dma_start(x_sb[:], one(x, b).rearrange("o (t p) d -> p (o t) d", p=P)).then_inc(x_loaded, 16)

            def load_side(b):
                sp.dma_start(side_raw[:],
                             one(side_t, b).rearrange("o (t p) k -> p (o t) k", p=P)).then_inc(side_loaded, 16)

            def load_ctx(b):
                sp.dma_start(scr_b[:].rearrange("p (t k) -> p t k", t=DT),
                             one(ctx_t, b).rearrange("o (t p) k -> p (o t) k", p=P)).then_inc(ctx_loaded, 16)

            def load_weight(i):
                n = names[i]
                if i >= 2:
                    sp.wait_ge(w_split, i - 1)
                sp.dma_start(stage[i % 2].rearrange("p (t n) -> p t n", t=DT),
                             w_src[n].rearrange("(t p) n -> p t n", p=P)).then_inc(w_loaded[i % 2], 16)

            load_x(0)
            load_weight(0)
            load_weight(1)
            load_side(0)
            load_ctx(0)
            load_mask(0, 0)
            load_mask(0, 1)
            sp.dma_start(wo_sb[:], wo_t.rearrange("(t p) n -> p t n", p=P)).then_inc(wo_loaded, 16)
            for i in range(2, len(names)):
                load_weight(i)

            def store(b):
                wait_apart(sp, "sp", out_done, b + 1)
                sp.dma_start(one(out, b).rearrange("o (t p) d -> p (o t) d", p=P), y[:]).then_inc(out_stored, 16)

            def batch(b, first=False, last=False):
                if not first:
                    load_mask(b, 1)
                if not last:
                    wait_apart(sp, "sp", kv_split, b + 1)
                    load_side(b + 1)
                load_mask(b, 2)
                if not last:
                    wait_apart(sp, "sp", xbo_done, b + 1)
                    load_x(b + 1)
                    if not first:
                        wait_apart(sp, "sp", xq_done, b)
                    load_ctx(b + 1)
                load_mask(b, 3)
                if not first:
                    store(b - 1)
                if not last:
                    load_mask(b + 1, 0)

            batch(0, first=True)
            with sp.Fori(1, B - 1) as b:
                batch(b)
            batch(B - 1, last=True)
            store(B - 1)
            sp.wait_ge(out_stored, 16 * B)

        @block.gpsimd
        def _(pool):
            for dst, src in (
                (qk_bias[:, 0, :], bq),
                (qk_bias[:, 1, :], bk),
                (qk_bias[:, 2, :], bgk),
                (bo_rows[:], bo.rearrange("(o n) -> o n", o=1).broadcast_to([P, D])),
                (fb_rows[:], ffn_bias.rearrange("(o n) -> o n", o=1).broadcast_to([P, D])),
                (s_in_col, s_in.rearrange("(o n) -> o n", o=1).broadcast_to([P, 1])),
                (s_k_col, s_k.rearrange("(o n) -> o n", o=1).broadcast_to([P, 1])),
                (xq[:].rearrange("p (t n) -> p t n", t=DT), ffn_w.rearrange("(t p) n -> p t n", p=P)),
                (y[0:1, :, :].rearrange("p a b -> p (a b)"), bv[0:512].rearrange("(o n) -> o n", o=1)),
                (xbo[0:1, :, :].rearrange("p a b -> p (a b)"), bv[512:1024].rearrange("(o n) -> o n", o=1)),
                (y[32:33, :, :].rearrange("p a b -> p (a b)"), bgv[0:512].rearrange("(o n) -> o n", o=1)),
                (xbo[32:33, :, :].rearrange("p a b -> p (a b)"), bgv[512:1024].rearrange("(o n) -> o n", o=1)),
            ):
                nc.gpsimd.dma_start(dst, src).then_inc(consts_loaded, 16)
            nc.gpsimd.memset(minus_half[:], -0.5)
            nc.gpsimd.memset(ident[:], 0.0).then_inc(ident_zero, 1)
            pool.wait_ge(ident_zero, 1)
            nc.gpsimd.affine_select(out=ident[:], in_=ident[:], compare_op=ALU.not_equal, fill=1.0, base=0,
                                    pattern=[[-1, P]], channel_multiplier=1).then_inc(ident_done, 1)

            def rstd_of(which, mv_ready, var_ready, rstd_ready, n):
                wait_apart(pool, "pool", mv_ready, QT * n)
                nc.gpsimd.tensor_scalar(var_eps[:, which, :], mv[:, which, :, 1], 1.0, LN_EPS,
                                        ALU.mult, ALU.add).then_inc(var_ready, 1)
                pool.wait_ge(var_ready, n)
                nc.gpsimd.tensor_tensor(rstd[:, which, :], var_eps[:, which, :], minus_half[:],
                                        ALU.pow).then_inc(rstd_ready, 1)

            def split_kv(n):
                pool.wait_ge(side_loaded, 16 * n)
                wait_apart(pool, "pool", ctx_loaded, 16 * n)
                both = ((slice(0, S), side_raw[:]), (slice(S, NK), scr_b[:].rearrange("p (t k) -> p t k", t=DT)))
                for keys, raw in both:
                    nc.gpsimd.tensor_scalar(kv_hi[:, :, keys], raw, 1.0, 0.0, ALU.mult, ALU.add).then_inc(kvhi_done, 1)
                for i, (keys, raw) in enumerate(both):
                    pool.wait_ge(kvhi_done, 2 * (n - 1) + i + 1)
                    last = nc.gpsimd.tensor_tensor(kv_lo[:, :, keys], raw, kv_hi[:, :, keys].bitcast(F32), ALU.subtract)
                last.then_inc(kv_split, 1)

            def copy_x(b):
                pool.wait_ge(z_done, QT * (b + 1))
                for t in range(QT):
                    i = nc.gpsimd.tensor_tensor(xbo[:, t, :], x_sb[:, t, :], bo_rows[:], ALU.add)
                i.then_inc(xbo_done, 1)

            def norm(g):
                wait_apart(pool, "pool", recip_done, g + 1)
                for t in range(QT):
                    nc.gpsimd.tensor_scalar(probs[:, slot_of(g), t, :], probs[:, slot_of(g), t, :],
                                            recips[:, slot_of(g), t:t + 1], 1.0,
                                            ALU.mult, ALU.mult).then_inc(norm_done, 1)

            def scale_quant_in(b):
                wait_apart(pool, "pool", z2_done, QT * (b + 1))
                nc.gpsimd.tensor_scalar(scr_a[:], z2[:], rs_in_col, 1.0, ALU.mult, ALU.mult).then_inc(v_done, 1)

            def finish(b, ff_freed):
                pool.wait_ge(misc_free, ff_freed)
                for t in range(QT):
                    nc.gpsimd.tensor_tensor(f1[:, t, :], f1[:, t, :], fb_rows[:], ALU.add).then_inc(f2_done, 1)
                pool.wait_ge(f2_done, QT * (b + 1))
                nc.gpsimd.tensor_tensor(y[:], y[:], f1[:], ALU.add).then_inc(out_done, 1)

            rstd_of(1, mv_x, var_x, rstd_x, 1)
            split_kv(1)
            pool.wait_ge(consts_done, 1)

            slot = [0]

            def slot_of(g):
                return slot[0]

            def batch(b, first=False, last=False):
                for h in range(H):
                    if not (last and h == H - 1):
                        slot[0] = (h + 1) % 2
                        norm(H * b + h + 1)
                    if h == 2:
                        if not first:
                            rstd_of(0, mv_y, var_y, rstd_y, b)
                        copy_x(b)
                    if h == 3 and not first:
                        scale_quant_in(b - 1)
                    if h == 7 and not last:
                        rstd_of(1, mv_x, var_x, rstd_x, b + 2)
                    if h == 8 and not first:
                        finish(b - 1, Chunks(b, first, last).through("ff_prev", 0))
                    if h == 10 and not last:
                        pool.wait_ge(misc_full, Chunks(b, first, last).through("v1", 3))
                        split_kv(b + 2)

            norm(0)
            batch(0, first=True)
            with pool.Fori(1, B - 1) as b:
                batch(b)
            batch(B - 1, last=True)
            rstd_of(0, mv_y, var_y, rstd_y, B)
            scale_quant_in(B - 1)
            finish(B - 1, TOTAL_CHUNKS)

        @block.tensor
        def _(pe):
            mm = nc.tensor.matmul

            def split_product(dst, a_hi, a_lo, b_hi, b_lo, more=False):
                n = 0
                for t in range(DT):
                    for a, c in ((a_hi, b_hi), (a_lo, b_hi), (a_hi, b_lo)):
                        n += 1
                        last = mm(dst, a(t), c(t), start=(n == 1), stop=(n == 3 * DT and not more))
                return last

            def chunk(c, place, first=False):
                kind, n = c.at[place]
                start = c.before(place)
                pe.wait_ge(misc_free, start)
                run_chunk(kind, n, c.b).then_inc(misc_full, 1)

            def run_chunk(kind, n, b):
                if kind == "q":
                    for p in range(GH // 2):
                        cols = slice((n * GH // 2 + p) * P, (n * GH // 2 + p + 1) * P)
                        last = split_product(ps_misc[:, p * S:(p + 1) * S],
                                             lambda t: w_hi["q"][:, t, cols], lambda t: w_lo["q"][:, t, cols],
                                             lambda t: zt_hi[:, t, :], lambda t: zt_lo[:, t, :])
                elif kind in ("k0", "k1"):
                    p = n * GH // 2 + int(kind[1])
                    cols = slice(p * P, (p + 1) * P)
                    for w, keys in (("k", slice(0, S)), ("gk", slice(S, NK))):
                        last = split_product(ps_misc[:, keys],
                                             lambda t: w_hi[w][:, t, cols], lambda t: w_lo[w][:, t, cols],
                                             lambda t: kv_hi[:, t, keys], lambda t: kv_lo[:, t, keys])
                elif kind in ("v0", "v1"):
                    half = int(kind[1])
                    w = ("v", "gv")[half]
                    cols = slice(n * GW, (n + 1) * GW)
                    for i in range(2):
                        keys = slice((2 * half + i) * P, (2 * half + i + 1) * P)
                        dst = ps_misc[:, i * GW:(i + 1) * GW]
                        split_product(dst, lambda t: kv_hi[:, t, keys], lambda t: kv_lo[:, t, keys],
                                      lambda t: w_hi[w][:, t, cols], lambda t: w_lo[w][:, t, cols], more=True)
                        last = mm(dst, vbias_ones[:], vbias[:, half, cols], start=False, stop=True)
                elif kind == "zt_next":
                    pe.wait_ge(z_done, QT * (b + 2))
                    last = transpose_z()
                elif kind == "wo_prev":
                    pe.wait_ge(wo_loaded, 16)
                    pe.wait_ge(o_done, H * b)
                    for t in range(QT):
                        for p in range(H // 2):
                            last = mm(ps_misc[:, t * D:(t + 1) * D], o_t[:, p, t * P:(t + 1) * P], wo_sb[:, p, :],
                                      start=(p == 0), stop=(p == H // 2 - 1))
                elif kind == "xq_prev":
                    pe.wait_ge(xq_done, b)
                    dst = ps_misc[:, 0:256].bitcast(BF16)
                    for t in range(DT):
                        for q in range(QT):
                            last = nc.tensor.transpose(dst[:, t * S + q * P:t * S + (q + 1) * P],
                                                       xq[:, q * D + t * P:q * D + (t + 1) * P], ident_bf[:])
                elif kind == "ff_prev":
                    for q in range(QT):
                        for t in range(DT):
                            last = mm(ps_misc[:, q * D:(q + 1) * D], xq_t[:, t, q * P:(q + 1) * P], ffn_q[:, t, :],
                                      start=(t == 0), stop=(t == DT - 1))
                return last

            def transpose_z():
                for t in range(DT):
                    for q in range(QT):
                        last = nc.tensor.transpose(ps_misc[:, t * S + q * P:t * S + (q + 1) * P],
                                                   scr_a[:, q * D + t * P:q * D + (t + 1) * P], ident[:])
                return last

            def scores(h, g, free=True):
                n, i = h // GH, h % GH
                if free:
                    pe.wait_ge(exp_done, QT * (g - 1))
                for t in range(QT):
                    dst = ps_scores[:, h % 2, t, :]
                    rows = slice(t * P, (t + 1) * P)
                    qh, ql = q_hi[:, n % 2, i, rows], q_lo[:, n % 2, i, rows]
                    kh, kl = k_hi[:, n % 2, i // 2, :], k_lo[:, n % 2, i // 2, :]
                    mm(dst, qh, kh, start=True, stop=False)
                    mm(dst, qh, kl, start=False, stop=False)
                    mm(dst, ql, kh, start=False, stop=False)
                    m = mask_sb[:, n % 2, (i * QT + t) * S:(i * QT + t + 1) * S].bitcast(FP8E5)
                    last = mm(dst[:, 0:S], mask_weight[:], m, start=False, stop=True)
                last.then_inc(scores_done, 1)

            def transposes(h, g, first=False):
                pe.wait_ge(norm_done, QT * (g + 1))
                for k in range(2):
                    if not first:
                        pe.wait_ge(ptlo_done, 2 * g - 1 + k)
                    for j in range(2):
                        for t in range(QT):
                            kt = 2 * k + j
                            last = nc.tensor.transpose(ps_pt[:, k, j, t * P:(t + 1) * P],
                                                       probs[:, h % 2, t, kt * P:(kt + 1) * P], ident[:])
                    last.then_inc(pt_full, 1)

            def outputs(h, g, first=False):
                pe.wait_ge(ptlo_done, 2 * (g + 1))
                if not first:
                    pe.wait_ge(o_done, g)
                n, i = h // GH, h % GH
                for kt in range(KT):
                    for pt in (pt_hi, pt_lo):
                        last = mm(ps_o[:, 0:S], v_hl[:, n % 2, kt, i, :], pt[:, h % 2, kt, :],
                                  start=(kt == 0 and pt is pt_hi), stop=(kt == KT - 1 and pt is pt_lo))
                last.then_inc(o_full, 1)

            pe.wait_ge(consts_done, 1)
            pe.wait_ge(z_done, QT)
            transpose_z().then_inc(misc_full, 1)
            pe.wait_ge(zeros_done, 2)
            for j, (kind, n) in enumerate(PROLOGUE[1:]):
                pe.wait_ge(misc_free, j + 1)
                pe.wait_ge(w_split, {"q": 1, "k0": 3, "k1": 3, "v0": 4, "v1": 5}[kind])
                if kind == "k0":
                    pe.wait_ge(kv_split, 1)
                run_chunk(kind, n, 0).then_inc(misc_full, 1)
            pe.wait_ge(misc_free, len(PROLOGUE))
            pe.wait_ge(mask_loaded[0], 16)
            scores(0, 0, free=False)
            scores(1, 1, free=False)

            def batch(b, first=False, last=False):
                c = Chunks(b, first, last)

                def do(place):
                    if place in c.at:
                        chunk(c, place)

                for h in range(H):
                    g = H * b + h
                    ahead = h + 2
                    if not (last and ahead >= H):
                        nxt = ahead // GH % NG
                        if ahead % GH == 0:
                            bb = b + ahead // H
                            pe.wait_ge(mask_loaded[nxt % 2], 16 * (2 * bb + nxt // 2 + 1))
                            pe.wait_ge(misc_free, c.through("k0", nxt))
                        if ahead % GH == 2:
                            if ahead == 2:
                                pass
                            else:
                                pe.wait_ge(misc_free, c.through("k1", nxt))
                        scores(ahead % H, g + 2)
                    do((h, "A"))
                    transposes(h, g, first and h == 0)
                    do((h, "B"))
                    if not (first and h == 0):
                        if (h - 1) % GH == 0:
                            n = (h - 1) // GH
                            if n > 0:
                                pe.wait_ge(misc_free, c.through("v1", n))
                        outputs((h - 1) % H, g - 1, first and h == 1)
                    do((h, "C"))

            batch(0, first=True)
            with pe.Fori(1, B - 1) as b:
                batch(b)
            batch(B - 1, last=True)
            outputs(H - 1, H * B - 1)
            for j, kind in enumerate(PREV):
                pe.wait_ge(misc_free, TAIL_AT + j)
                run_chunk(kind, 0, B).then_inc(misc_full, 1)

        @block.scalar
        def _(act):
            act.wait_ge(zeros_done, 2)

            def split_hi(kind, n):
                r = n % 2
                if kind == "q":
                    for p in range(GH // 2):
                        for e in range(2):
                            rows = slice(e * DK, (e + 1) * DK)
                            last = nc.scalar.activation(q_hi[rows, r, 2 * p + e, :], ps_misc[rows, p * S:(p + 1) * S],
                                                        ACT.Identity, bias=qk_bias[rows, 0, n * 2 + p:n * 2 + p + 1])
                elif kind in ("k0", "k1"):
                    p = int(kind[1])
                    for j in range(2):
                        last = nc.scalar.activation(k_hi[:, r, p, j * S:(j + 1) * S], ps_misc[:, j * S:(j + 1) * S],
                                                    ACT.Identity, bias=qk_bias[:, 1 + j, n * 2 + p:n * 2 + p + 1])
                elif kind in ("v0", "v1"):
                    half = int(kind[1])
                    last = nc.scalar.copy(v_hl[:, r, 2 * half:2 * half + 2, :, 0:DK].rearrange("p k h d -> p (k h) d"),
                                          ps_misc[:].rearrange("p (k d) -> p k d", d=DK))
                else:
                    last = nc.scalar.copy(zt_hi[:].rearrange("p t s -> p (t s)"), ps_misc[:])
                last.then_inc(hi_done, 1)

            def chunk(kind, n, before, b):
                act.wait_ge(misc_full, before + 1)
                if kind in SPLIT:
                    split_hi(kind, n)
                elif kind == "xq_prev":
                    nc.scalar.copy(xq_t[:].rearrange("p t s -> p (t s)"),
                                   ps_misc[:, 0:256].bitcast(BF16)).then_inc(misc_free, 1)
                elif kind == "ff_prev":
                    nc.scalar.activation(f1[:].rearrange("p t d -> p (t d)"), ps_misc[:], ACT.Copy,
                                         scale=ss_col).then_inc(misc_free, 1)

            def exps(h, g, free=True):
                act.wait_ge(min_done, g + 1)
                if free:
                    act.wait_ge(pt_full, 2 * (g - 1))
                for t in range(QT):
                    nc.scalar.activation(probs[:, h % 2, t, :], ps_scores[:, h % 2, t, :], ACT.Exp,
                                         bias=neg_max[:, h % 2, t:t + 1], scale=-1.0,
                                         accum_out=sums[:, h % 2, t:t + 1]).then_inc(exp_done, 1)

            def pt_his(h, g, free=True):
                for k in range(2):
                    act.wait_ge(pt_full, 2 * g + k + 1)
                    if free and k == 0:
                        act.wait_ge(o_full, g - 1)
                    nc.scalar.copy(pt_hi[:, h % 2, 2 * k:2 * k + 2, :], ps_pt[:, k, :, :]).then_inc(pthi_done, 1)

            def o_los(h, g, first=False):
                act.wait_ge(o_full, g + 1)
                if not first:
                    act.wait_ge(o_done, g)
                nc.scalar.copy(o_lo[:], ps_o[DK:P, 0:S]).then_inc(olo_done, 1)

            for j, (kind, n) in enumerate(PROLOGUE):
                if j == 1:
                    act.wait_ge(consts_done, 1)
                chunk(kind, n, j, 0)
            exps(0, 0, free=False)

            def batch(b, first=False, last=False):
                c = Chunks(b, first, last)

                def do(place):
                    if place in c.at:
                        chunk(*c.at[place], c.before(place), b)

                for h in range(H):
                    g = H * b + h
                    if not (last and h == H - 1):
                        exps((h + 1) % H, g + 1, free=not (first and h == 0))
                    do((h, "A"))
                    pt_his(h, g, free=not (first and h < 2))
                    do((h, "B"))
                    if not (first and h == 0):
                        o_los((h - 1) % H, g - 1, first and h == 1)
                    do((h, "C"))

            batch(0, first=True)
            with act.Fori(1, B - 1) as b:
                batch(b)
            batch(B - 1, last=True)
            o_los(H - 1, H * B - 1)
            for j, kind in enumerate(PREV):
                if kind != "wo_prev":
                    chunk(kind, 0, TAIL_AT + j, B)

        @block.vector
        def _(dve):
            V = nc.vector

            def e4m3fn(v, t, dst, n):
                base = QUANT_STEPS * n - QUANT_STEPS

                def step(i, ins):
                    ins.then_inc(quant_chain, 1)
                    dve.wait_ge(quant_chain, base + i)

                step(1, V.tensor_scalar(t.bitcast(U32), v.bitcast(U32), 0x7F800000, None, ALU.bitwise_and))
                step(2, V.tensor_scalar(t, t, E4_MIN_NORMAL, E4_MAGIC, ALU.max, ALU.mult))
                step(3, V.tensor_tensor(v, v, t, ALU.add))
                step(4, V.tensor_tensor(v, v, t, ALU.subtract))
                step(5, V.scalar_tensor_tensor(out=t, in0=v, scalar=E4_OVERFLOW, in1=v, op0=ALU.mult, op1=ALU.mult))
                return V.scalar_tensor_tensor(out=dst, in0=t, scalar=0.0, in1=v, op0=ALU.mult, op1=ALU.add)

            def split_lo(kind, n):
                r = n % 2
                if kind == "q":
                    for p in range(GH // 2):
                        for e in range(2):
                            rows = slice(e * DK, (e + 1) * DK)
                            last = V.scalar_tensor_tensor(
                                out=q_lo[rows, r, 2 * p + e, :], in0=ps_misc[rows, p * S:(p + 1) * S],
                                scalar=qk_bias[rows, 0, n * 2 + p:n * 2 + p + 1],
                                in1=q_hi[rows, r, 2 * p + e, :].bitcast(F32), op0=ALU.add, op1=ALU.subtract)
                elif kind in ("k0", "k1"):
                    p = int(kind[1])
                    for j in range(2):
                        last = V.scalar_tensor_tensor(
                            out=k_lo[:, r, p, j * S:(j + 1) * S], in0=ps_misc[:, j * S:(j + 1) * S],
                            scalar=qk_bias[:, 1 + j, n * 2 + p:n * 2 + p + 1],
                            in1=k_hi[:, r, p, j * S:(j + 1) * S].bitcast(F32), op0=ALU.add, op1=ALU.subtract)
                elif kind in ("v0", "v1"):
                    half = int(kind[1])
                    v = v_hl[:, r, 2 * half:2 * half + 2, :, :].rearrange("p k h d -> p (k h) d")
                    last = V.tensor_tensor(v[:, :, DK:2 * DK], ps_misc[:].rearrange("p (k d) -> p k d", d=DK),
                                           v[:, :, 0:DK].bitcast(F32), ALU.subtract)
                else:
                    last = V.tensor_tensor(zt_lo[:].rearrange("p t s -> p (t s)"), ps_misc[:],
                                           zt_hi[:].rearrange("p t s -> p (t s)").bitcast(F32), ALU.subtract)
                last.then_inc(misc_free, 1)

            def moments(which, src, bn_ready, mv_ready, n):
                for t in range(QT):
                    V.bn_stats(stats[:, which, t, :], src[:, t, :]).then_inc(bn_ready, 1)
                for t in range(QT):
                    wait_apart(dve, "dve", bn_ready, QT * (n - 1) + t + 1)
                    V.bn_aggr(mv[:, which, t, :], stats[:, which, t, :]).then_inc(mv_ready, 1)

            def normalise(which, dst, src, done):
                for t in range(QT):
                    V.tensor_scalar(dst[:, t * D:(t + 1) * D], src[:, t, :], mv[:, which, t, 0:1],
                                    rstd[:, which, t:t + 1], ALU.subtract, ALU.mult).then_inc(done, 1)

            def chunk(kind, n, before, hi_before, b):
                if kind in SPLIT:
                    dve.wait_ge(hi_done, hi_before + 1)
                    split_lo(kind, n)
                elif kind == "wo_prev":
                    dve.wait_ge(misc_full, before + 1)
                    dve.wait_ge(xbo_done, b)
                    if not (isinstance(b, int) and b == 1):
                        dve.wait_ge(out_stored, 16 * (b - 1))
                    V.tensor_tensor(y[:].rearrange("p t d -> p (t d)"), ps_misc[:],
                                    xbo[:].rearrange("p t d -> p (t d)"), ALU.add).then_inc(misc_free, 1)
                    dve.wait_ge(misc_free, before + 1)
                    moments(0, y, bn_y, mv_y, b)

            def mins(h, g):
                dve.wait_ge(scores_done, g + 1)
                V.tensor_reduce(neg_max[:, h % 2, :], ps_scores[:, h % 2, :, :], AX_X, ALU.min).then_inc(min_done, 1)

            def recip(h, g):
                dve.wait_ge(exp_done, QT * (g + 1))
                V.reciprocal(recips[:, h % 2, :], sums[:, h % 2, :]).then_inc(recip_done, 1)

            def pt_los(h, g):
                for k in range(2):
                    dve.wait_ge(pthi_done, 2 * g + k + 1)
                    V.tensor_tensor(pt_lo[:, h % 2, 2 * k:2 * k + 2, :], ps_pt[:, k, :, :],
                                    pt_hi[:, h % 2, 2 * k:2 * k + 2, :].bitcast(F32),
                                    ALU.subtract).then_inc(ptlo_done, 1)

            def o_adds(h, g):
                dve.wait_ge(olo_done, g + 1)
                e = h % 2
                V.tensor_tensor(o_t[e * DK:(e + 1) * DK, h // 2, :], ps_o[0:DK, 0:S], o_lo[:],
                                ALU.add).then_inc(o_done, 1)

            dve.wait_ge(x_loaded, 16)
            moments(1, x_sb, bn_x, mv_x, 1)
            V.memzero(q_hi[:].rearrange("p a b c -> p (a b c)").bitcast(F32)).then_inc(zeros_done, 1)
            V.memzero(q_lo[:].rearrange("p a b c -> p (a b c)").bitcast(F32)).then_inc(zeros_done, 1)
            dve.wait_ge(rstd_x, 1)
            normalise(1, scr_a, x_sb, z_done)
            dve.wait_ge(ident_done, 1)
            V.tensor_copy(ident_bf[:], ident[:])
            V.tensor_scalar(mask_weight[:], ident[:], MASK_WEIGHT, None, ALU.mult).then_inc(prep_chain, 1)
            dve.wait_ge(consts_loaded, 16 * 12)
            chain = [1]

            def link(ins):
                chain[0] += 1
                ins.then_inc(prep_chain, 1)
                dve.wait_ge(prep_chain, chain[0])

            link(V.memset(vbias[:], 0.0))
            link(V.memset(vbias_ones[:], 0.0))
            for row in (0, 32, 64):
                link(V.memset(vbias_ones[row:row + 1, :], 1.0))
            link(V.tensor_scalar(qk_bias[:, 0, :], qk_bias[:, 0, :], SCORE_SCALE, None, ALU.mult))
            link(V.reciprocal(scales[:, 2:4], scales[:, 0:2]))
            link(V.tensor_tensor(ss_col, s_in_col, s_k_col, ALU.mult))
            for half in range(2):
                for i, src in enumerate((y, xbo)):
                    row = src[half * 32:half * 32 + 1, :, :].rearrange("p a b -> p (a b)")
                    cols = slice(i * 512, (i + 1) * 512)
                    rest = ps_o[half * 32:half * 32 + 1, :]
                    part = z2[half * 32:half * 32 + 1, :]
                    link(V.tensor_copy(part, row))
                    link(V.tensor_copy(vbias[0:1, half, cols], part))
                    link(V.tensor_tensor(rest, row, part, ALU.subtract))
                    link(V.tensor_copy(part, rest))
                    link(V.tensor_copy(vbias[32:33, half, cols], part))
                    link(V.tensor_tensor(rest, rest, part, ALU.subtract))
                    link(V.tensor_copy(vbias[64:65, half, cols], rest))
            v_w = xbo[:].rearrange("p a b -> p (a b)")
            t_w = y[:].rearrange("p a b -> p (a b)")
            link(V.tensor_scalar(v_w, xq[:], rs_k_col, None, ALU.mult))
            e4m3fn(v_w, t_w, ffn_q[:].rearrange("p t n -> p (t n)"), 1).then_inc(consts_done, 1)

            def split_weight(i):
                n = names[i]
                scale = SCORE_SCALE if n == "q" else 1.0
                raw = stage[i % 2]
                hi = w_hi[n][:].rearrange("p t n -> p (t n)")
                dve.wait_ge(w_loaded[i % 2], 16 * (i // 2 + 1))
                V.tensor_scalar(hi, raw, scale, None, ALU.mult).then_inc(w_hi_done, 1)
                dve.wait_ge(w_hi_done, i + 1)
                V.scalar_tensor_tensor(out=w_lo[n][:].rearrange("p t n -> p (t n)"), in0=raw, scalar=scale,
                                       in1=hi.bitcast(F32), op0=ALU.mult, op1=ALU.subtract).then_inc(w_split, 1)

            def prologue_chunk(j):
                chunk(*PROLOGUE[j], j, j, 0)

            prologue_chunk(0)
            split_weight(0)
            prologue_chunk(1)
            split_weight(1)
            split_weight(2)
            prologue_chunk(2)
            prologue_chunk(3)
            split_weight(3)
            prologue_chunk(4)
            split_weight(4)
            prologue_chunk(5)
            mins(0, 0)
            recip(0, 0)

            def quantise(b):
                dve.wait_ge(v_done, b)
                e4m3fn(scr_a[:], scr_b[:], xq[:], b + 1).then_inc(xq_done, 1)

            def normalise_y(b):
                dve.wait_ge(rstd_y, b)
                normalise(0, z2, y, z2_done)

            def batch(b, first=False, last=False):
                c = Chunks(b, first, last)

                def do(place):
                    if place in c.at:
                        chunk(*c.at[place], c.before(place), c.before(place, SPLIT), b)

                for h in range(H):
                    g = H * b + h
                    if not (last and h == H - 1):
                        mins((h + 1) % H, g + 1)
                    do((h, "A"))
                    if not (last and h == H - 1):
                        recip((h + 1) % H, g + 1)
                    pt_los(h, g)
                    do((h, "B"))
                    if not (first and h == 0):
                        o_adds((h - 1) % H, g - 1)
                    do((h, "C"))
                    if h == 3 and not first:
                        normalise_y(b)
                    if h == 4 and not first:
                        quantise(b)
                    if h == 6 and not last:
                        dve.wait_ge(x_loaded, 16 * (b + 2))
                        moments(1, x_sb, bn_x, mv_x, b + 2)
                    if h == 8 and not last:
                        dve.wait_ge(rstd_x, b + 2)
                        normalise(1, scr_a, x_sb, z_done)

            batch(0, first=True)
            with dve.Fori(1, B - 1) as b:
                batch(b)
            batch(B - 1, last=True)
            o_adds(H - 1, H * B - 1)
            chunk("wo_prev", 0, TAIL_AT, 0, B)
            normalise_y(B)
            quantise(B)


def kernel(**inputs):
    import numpy as np
    import concourse.bacc as bacc
    from concourse.bass_utils import run_bass_kernel_spmd

    a = {k: np.asarray(v) for k, v in inputs.items()}
    w = {k[len("L0_xattn_"):]: v for k, v in a.items() if k.startswith("L0_xattn_")}
    m = a["mask_Bx16xSxS_bk1"].reshape(B, H, QT, P, S).transpose(0, 3, 1, 2, 4).reshape(B, P, H * QT * S)

    def columns(name):
        return w[name].reshape(-1, P).T

    arrays = {
        "x": a["x"],
        "side_t": a["fside_BxSxS_0"].transpose(0, 2, 1),
        "ctx_t": a["ctx_1024"].transpose(0, 2, 1),
        "mask": m,
        "wq_t": w["Wq"].T, "bq": columns("bq"), "wk_t": w["Wk"].T, "bk": columns("bk"), "wgk_t": w["Wgk"].T, "bgk": columns("bgk"),
        "wv_t": w["Wv"].T, "bv": w["bv"], "wgv_t": w["Wgv"].T, "bgv": w["bgv"], "wo_t": w["Wo"].T, "bo": w["bo"],
        "ffn_w": a["L0_ffn_kernel"], "s_in": a["L0_ffn_input_scale"], "s_k": a["L0_ffn_kernel_scale"],
        "ffn_bias": a["L0_ffn_bias"],
    }
    arrays = {f"{k}_dram": np.ascontiguousarray(v) for k, v in arrays.items()}
    nc = bacc.Bacc("TRN2", target_bir_lowering=False, num_devices=1)
    args = [nc.dram_tensor(k, v.shape, mybir.dt.from_np(v.dtype), kind="ExternalInput").ap()
            for k, v in arrays.items()]
    args.append(nc.dram_tensor("out_dram", (B, S, D), F32, kind="ExternalOutput").ap())
    xattn_ffn_kernel(nc, *args)
    r = run_bass_kernel_spmd(nc, [arrays], core_ids=[0])
    return r.results[0]["out_dram"]
```

```python
from contextlib import ExitStack

import concourse.bass as bass
from concourse import mybir

F32 = mybir.dt.float32
F32R = mybir.dt.float32r
BF16 = mybir.dt.bfloat16
FP8E5 = mybir.dt.float8e5
U8 = mybir.dt.uint8
U32 = mybir.dt.uint32
ALU = mybir.AluOpType
ACT = mybir.ActivationFunctionType
AX_X = mybir.AxisListType.X

P = 128
B, S, D, H = 32, 256, 256, 16
DK = 64
NK = 2 * S
QT = S // P
DT = D // P
KT = NK // P
GH = 4
NG = H // GH
GW = GH * DK
SCORE_SCALE = -1.0 / DK ** 0.5
LN_EPS = 1e-5
MASK_WEIGHT = 2.0 ** 116
E4_MAGIC = 1.5 * 2.0 ** 20
E4_MIN_NORMAL = 2.0 ** -6
E4_OVERFLOW = 1.69e33

PLACES = {
    (1, "A"): ("wo_prev", 0), (6, "B"): ("xq_prev", 0), (7, "B"): ("ff_prev", 0), (11, "A"): ("zt_next", 0),
    (0, "A"): ("q", 1), (0, "B"): ("k0", 1), (2, "A"): ("k1", 1), (2, "B"): ("v0", 1), (3, "A"): ("v1", 1),
    (4, "A"): ("q", 2), (4, "B"): ("k0", 2), (5, "A"): ("k1", 2), (6, "A"): ("v0", 2), (7, "A"): ("v1", 2),
    (8, "A"): ("q", 3), (8, "B"): ("k0", 3), (9, "A"): ("k1", 3), (9, "B"): ("v0", 3), (10, "A"): ("v1", 3),
    (12, "A"): ("q", 0), (12, "B"): ("k0", 0), (13, "A"): ("k1", 0), (14, "A"): ("v0", 0), (15, "A"): ("v1", 0),
}
SLOT_ORDER = [(h, place) for h in range(H) for place in "AB"]
PROLOGUE = [("zt_next", 0), ("q", 0), ("k0", 0), ("k1", 0), ("v0", 0), ("v1", 0)]
PREV = ("wo_prev", "xq_prev", "ff_prev")
FIRST_PLACE = (0, "A")


def chunks_of(first, last):
    def kept(place, chunk):
        kind, group = chunk
        if first and kind in PREV:
            return False
        return not (last and (kind == "zt_next" or place[0] >= 12))
    return {place: PLACES[place] for place in SLOT_ORDER if place in PLACES and kept(place, PLACES[place])}


FIRST = list(chunks_of(True, False).values())
STEADY = list(chunks_of(False, False).values())
KV = ("k0", "k1", "v0", "v1")
ZQ = ("zt_next", "q")


assert (H - 1, "B") not in PLACES


def count_before(b, kinds):
    per = sum(kind in kinds for kind, _ in STEADY)
    head = sum(kind in kinds for kind, _ in PROLOGUE)
    if isinstance(b, int) and b == 0:
        return head
    return per * b + (head + sum(kind in kinds for kind, _ in FIRST) - per)


ALL_KINDS = KV + ZQ + PREV


TAIL_AT = count_before(B - 1, ALL_KINDS) + len(chunks_of(False, True))
TOTAL_CHUNKS = TAIL_AT + len(PREV)


KV_TURN = {chunk: i % 2 for i, chunk in enumerate(chunk for chunk in STEADY if chunk[0] in KV)}


class Chunks:

    def __init__(self, b, first=False, last=False):
        self.b, self.at = b, chunks_of(first, last)
        self.order = list(self.at)

    def before(self, place, kinds=ALL_KINDS):
        n = sum(self.at[p][0] in kinds for p in self.order[:self.order.index(place)])
        return count_before(self.b, kinds) + n

    def through(self, kind, group, kinds=ALL_KINDS):
        for p in self.order:
            if self.at[p] == (kind, group):
                return self.before(p, kinds) + 1
        raise KeyError(kind)


def xattn_ffn_kernel(nc, x, side_t, ctx_t, mask, wq_t, bq, wk_t, bk, wgk_t, bgk, wv_t, bv, wgv_t, bgv,
                     wo_t, bo, ffn_w, s_in, s_k, ffn_bias, out):
    with ExitStack() as ctx:
        def sb(name, shape, dt):
            return ctx.enter_context(nc.sbuf_tensor(name, shape, dt))

        def psum(name, shape, dt=F32):
            return ctx.enter_context(nc.psum_tensor(name, shape, dt))

        def sem(name):
            return ctx.enter_context(nc.semaphore(name))

        names = ["q", "k", "gk", "v", "gv"]
        w_hi = {n: sb(f"w{n}_hi", [P, DT, H * DK], F32R) for n in names}
        w_lo = {n: sb(f"w{n}_lo", [P, DT, H * DK], F32R) for n in names}
        wo_sb = sb("wo_sb", [P, H * DK // P, D], F32)
        ffn_q = sb("ffn_q", [P, DT, D], BF16)
        vbias = sb("vbias", [P, 2, H * DK], BF16)
        vbias_ones = sb("vbias_ones", [P, P], BF16)
        qk_bias = sb("qk_bias", [P, 3, H * DK // P], F32)
        bo_rows = sb("bo_rows", [P, D], F32)
        fb_rows = sb("fb_rows", [P, D], BF16)
        scales = sb("scales", [P, 8], F32)
        ident = sb("ident", [P, P], F32)
        ident_bf = sb("ident_bf", [P, P], BF16)
        mask_weight = sb("mask_weight", [P, P], BF16)

        side_raw = sb("side_raw", [P, DT, S], F32)
        kv_hi = sb("kv_hi", [P, DT, NK], F32R)
        kv_lo = sb("kv_lo", [P, DT, NK], F32R)
        x_sb = sb("x_sb", [P, QT, D], F32)
        xbo = sb("xbo", [P, QT, D], F32)
        zt_hi = sb("zt_hi", [P, DT, S], F32R)
        zt_lo = sb("zt_lo", [P, DT, S], F32R)
        o_t = sb("o_t", [P, H // 2, S], F32)
        y = sb("y", [P, QT, D], F32)
        scr_a = sb("scr_a", [P, QT * D], F32)
        scr_b = sb("scr_b", [P, QT * D], F32)
        z2 = sb("z2", [P, QT * D], BF16)
        xq = sb("xq", [P, QT * D], BF16)
        xq_t = z2[:].rearrange("p (t s) -> p t s", t=DT)
        f1 = xq[:].rearrange("p (t d) -> p t d", t=QT)
        stats = sb("stats", [P, 2, QT, 6], F32)
        mv = sb("mv", [P, 2, QT, 2], F32)
        var_eps = sb("var_eps", [P, 2, QT], F32)
        rstd = sb("rstd", [P, 2, QT], F32)
        minus_half = sb("minus_half", [P, QT], F32)

        q_hi = sb("q_hi", [P, 2, GH, S], F32R)
        q_lo = sb("q_lo", [P, 2, GH, S], F32R)
        k_hi = sb("k_hi", [P, 2, GH // 2, NK], F32R)
        k_lo = sb("k_lo", [P, 2, GH // 2, NK], F32R)
        v_hl = sb("v_hl", [P, 2, KT, GH, 2 * DK], F32R)
        mask_sb = sb("mask_sb", [P, 2, GH * QT * S], U8)
        kv_out = sb("kv_out", [P, 2, 512], F32)
        zq_out = sb("zq_out", [P, 512], F32)
        probs = sb("probs", [P, 2, QT, NK], F32)
        pt_hi = sb("pt_hi", [P, 2, KT, S], F32R)
        pt_lo = sb("pt_lo", [P, 2, KT, S], F32R)
        neg_max = sb("neg_max", [P, 2, QT], F32)
        sums = sb("sums", [P, 2, QT], F32)
        recips = sb("recips", [P, 2, QT], F32)
        o_lo = sb("o_lo", [DK, S], F32)

        ps_scores = psum("ps_scores", [P, 2, QT, NK])
        ps_pt = psum("ps_pt", [P, 2, 2, S])
        ps_o = psum("ps_o", [P, 512])
        ps_misc = psum("ps_misc", [P, 512])

        w_loaded = [sem("w_loaded0"), sem("w_loaded1")]
        w_split = sem("w_split")
        w_hi_done = sem("w_hi_done")
        consts_loaded = sem("consts_loaded")
        wo_loaded = sem("wo_loaded")
        ident_zero = sem("ident_zero")
        ident_done = sem("ident_done")
        consts_done = sem("consts_done")
        ffn_chain = sem("ffn_chain")
        prep_chain = sem("prep_chain")
        zeros_done = sem("zeros_done")
        mask_loaded = [sem("mask_loaded0"), sem("mask_loaded1")]
        side_loaded = sem("side_loaded")
        ctx_loaded = sem("ctx_loaded")
        x_loaded = sem("x_loaded")
        out_stored = sem("out_stored")
        scores_done = sem("scores_done")
        pt_full = sem("pt_full")
        o_full = sem("o_full")
        misc_full = sem("misc_full")
        misc_free = sem("misc_free")
        kv_hi_part = sem("kv_hi_part")
        kv_ready = sem("kv_ready")
        zq_hi_part = sem("zq_hi_part")
        zq_ready = sem("zq_ready")
        exp_done = sem("exp_done")
        pthi_done = sem("pthi_done")
        ptlo_done = sem("ptlo_done")
        olo_done = sem("olo_done")
        o_done = sem("o_done")
        min_done = sem("min_done")
        recip_done = sem("recip_done")
        norm_done = sem("norm_done")
        kvhi_done = sem("kvhi_done")
        kv_split = sem("kv_split")
        xbo_done = sem("xbo_done")
        bn_x = sem("bn_x")
        mv_x = sem("mv_x")
        var_x = sem("var_x")
        rstd_x = sem("rstd_x")
        z_done = sem("z_done")
        bn_y = sem("bn_y")
        mv_y = sem("mv_y")
        var_y = sem("var_y")
        rstd_y = sem("rstd_y")
        z2_done = sem("z2_done")
        v_done = sem("v_done")
        quant_chain = sem("quant_chain")
        xq_done = sem("xq_done")
        f2_done = sem("f2_done")
        out_done = sem("out_done")

        QUANT_STEPS = 5
        w_src = {"q": wq_t, "k": wk_t, "gk": wgk_t, "v": wv_t, "gv": wgv_t}
        stage = [probs[:].rearrange("p a b c -> p (a b c)"), o_t[:].rearrange("p a b -> p (a b)")]
        s_in_col, s_k_col, rs_in_col, rs_k_col, ss_col = (scales[:, i:i + 1] for i in range(5))

        block = ctx.enter_context(nc.Block())

        waits_passed = {e: sem(f"waits_passed_{e}") for e in ("sp", "pool", "dve")}

        def wait_apart(engine, name, semaphore, value):
            engine.wait_ge(semaphore, value)
            engine.sem_inc(waits_passed[name], 1)

        @block.sync
        def _(sp):
            def load_mask(b, n):
                if not (isinstance(b, int) and b == 0 and n < 2):
                    wait_apart(sp, "sp", scores_done, H * b + GH * (n - 1))
                src = one(mask, b).rearrange("o p n -> (o p) n")
                sp.dma_start(mask_sb[:, n % 2, :],
                             src[:, n * GH * QT * S:(n + 1) * GH * QT * S]).then_inc(mask_loaded[n % 2], 16)

            def one(ap, b):
                return ap[b:b + 1] if isinstance(b, int) else ap[bass.ds(b, 1)]

            def load_x(b):
                sp.dma_start(x_sb[:], one(x, b).rearrange("o (t p) d -> p (o t) d", p=P)).then_inc(x_loaded, 16)

            def load_side(b):
                sp.dma_start(side_raw[:],
                             one(side_t, b).rearrange("o (t p) k -> p (o t) k", p=P)).then_inc(side_loaded, 16)

            def load_ctx(b):
                sp.dma_start(scr_b[:].rearrange("p (t k) -> p t k", t=DT),
                             one(ctx_t, b).rearrange("o (t p) k -> p (o t) k", p=P)).then_inc(ctx_loaded, 16)

            def load_weight(i):
                n = names[i]
                if i >= 2:
                    sp.wait_ge(w_split, i - 1)
                sp.dma_start(stage[i % 2].rearrange("p (t n) -> p t n", t=DT),
                             w_src[n].rearrange("(t p) n -> p t n", p=P)).then_inc(w_loaded[i % 2], 16)

            load_x(0)
            load_weight(0)
            load_weight(1)
            load_side(0)
            load_ctx(0)
            load_mask(0, 0)
            load_mask(0, 1)
            sp.dma_start(wo_sb[:], wo_t.rearrange("(t p) n -> p t n", p=P)).then_inc(wo_loaded, 16)
            for i in range(2, len(names)):
                load_weight(i)

            def store(b):
                wait_apart(sp, "sp", out_done, b + 1)
                sp.dma_start(one(out, b).rearrange("o (t p) d -> p (o t) d", p=P), y[:]).then_inc(out_stored, 16)

            def batch(b, first=False, last=False):
                if not first:
                    load_mask(b, 1)
                if not last:
                    wait_apart(sp, "sp", kv_split, 2 * (b + 1))
                    load_side(b + 1)
                load_mask(b, 2)
                if not last:
                    wait_apart(sp, "sp", xbo_done, b + 1)
                    load_x(b + 1)
                    if not first:
                        wait_apart(sp, "sp", xq_done, b)
                    load_ctx(b + 1)
                load_mask(b, 3)
                if not first:
                    store(b - 1)
                if not last:
                    load_mask(b + 1, 0)

            batch(0, first=True)
            with sp.Fori(1, B - 1) as b:
                batch(b)
            batch(B - 1, last=True)
            store(B - 1)
            sp.wait_ge(out_stored, 16 * B)

        @block.gpsimd
        def _(pool):
            for dst, src in (
                (qk_bias[:, 0, :], bq),
                (qk_bias[:, 1, :], bk),
                (qk_bias[:, 2, :], bgk),
                (bo_rows[:], bo.rearrange("(o n) -> o n", o=1).broadcast_to([P, D])),
                (fb_rows[:], ffn_bias.rearrange("(o n) -> o n", o=1).broadcast_to([P, D])),
                (s_in_col, s_in.rearrange("(o n) -> o n", o=1).broadcast_to([P, 1])),
                (s_k_col, s_k.rearrange("(o n) -> o n", o=1).broadcast_to([P, 1])),
                (xq[:].rearrange("p (t n) -> p t n", t=DT), ffn_w.rearrange("(t p) n -> p t n", p=P)),
                (y[0:1, :, :].rearrange("p a b -> p (a b)"), bv[0:512].rearrange("(o n) -> o n", o=1)),
                (xbo[0:1, :, :].rearrange("p a b -> p (a b)"), bv[512:1024].rearrange("(o n) -> o n", o=1)),
                (y[32:33, :, :].rearrange("p a b -> p (a b)"), bgv[0:512].rearrange("(o n) -> o n", o=1)),
                (xbo[32:33, :, :].rearrange("p a b -> p (a b)"), bgv[512:1024].rearrange("(o n) -> o n", o=1)),
            ):
                nc.gpsimd.dma_start(dst, src).then_inc(consts_loaded, 16)
            nc.gpsimd.memset(minus_half[:], -0.5)
            nc.gpsimd.memset(ident[:], 0.0).then_inc(ident_zero, 1)
            pool.wait_ge(ident_zero, 1)
            nc.gpsimd.affine_select(out=ident[:], in_=ident[:], compare_op=ALU.not_equal, fill=1.0, base=0,
                                    pattern=[[-1, P]], channel_multiplier=1).then_inc(ident_done, 1)

            def rstd_of(which, mv_ready, var_ready, rstd_ready, n):
                wait_apart(pool, "pool", mv_ready, QT * n)
                nc.gpsimd.tensor_scalar(var_eps[:, which, :], mv[:, which, :, 1], 1.0, LN_EPS,
                                        ALU.mult, ALU.add).then_inc(var_ready, 1)
                pool.wait_ge(var_ready, n)
                nc.gpsimd.tensor_tensor(rstd[:, which, :], var_eps[:, which, :], minus_half[:],
                                        ALU.pow).then_inc(rstd_ready, 1)

            def split_rows(n, part):
                loaded = (side_loaded, ctx_loaded)[part]
                raw = (side_raw[:], scr_b[:].rearrange("p (t k) -> p t k", t=DT))[part]
                keys = slice(part * S, (part + 1) * S)
                wait_apart(pool, "pool", loaded, 16 * n)
                nc.gpsimd.tensor_scalar(kv_hi[:, :, keys], raw, 1.0, 0.0, ALU.mult, ALU.add).then_inc(kvhi_done, 1)
                pool.wait_ge(kvhi_done, 2 * (n - 1) + part + 1)
                nc.gpsimd.tensor_tensor(kv_lo[:, :, keys], raw, kv_hi[:, :, keys].bitcast(F32),
                                        ALU.subtract).then_inc(kv_split, 1)

            def copy_x(b):
                pool.wait_ge(z_done, QT * (b + 1))
                for t in range(QT):
                    i = nc.gpsimd.tensor_tensor(xbo[:, t, :], x_sb[:, t, :], bo_rows[:], ALU.add)
                i.then_inc(xbo_done, 1)

            def split_chunk(kind, n, copied, before):
                src = kv_out[:, KV_TURN[kind, n], :]
                r = n % 2
                if kind in ("k0", "k1"):
                    hi, lo = k_hi[:, r, int(kind[1]), :], k_lo[:, r, int(kind[1]), :]
                else:
                    half = int(kind[1])
                    v = v_hl[:, r, 2 * half:2 * half + 2, :, :].rearrange("p k h d -> p (k h) d")
                    src = src.rearrange("p (k d) -> p k d", d=DK)
                    hi, lo = v[:, :, 0:DK], v[:, :, DK:2 * DK]
                wait_apart(pool, "pool", misc_free, copied)
                nc.gpsimd.tensor_scalar(hi, src, 1.0, 0.0, ALU.mult, ALU.add).then_inc(kv_hi_part, 1)
                pool.wait_ge(kv_hi_part, before + 1)
                nc.gpsimd.tensor_tensor(lo, src, hi.bitcast(F32), ALU.subtract).then_inc(kv_ready, 1)

            def norm(g):
                wait_apart(pool, "pool", recip_done, g + 1)
                for t in range(QT):
                    nc.gpsimd.tensor_scalar(probs[:, slot_of(g), t, :], probs[:, slot_of(g), t, :],
                                            recips[:, slot_of(g), t:t + 1], 1.0,
                                            ALU.mult, ALU.mult).then_inc(norm_done, 1)

            def scale_quant_in(b):
                wait_apart(pool, "pool", z2_done, QT * (b + 1))
                nc.gpsimd.tensor_scalar(scr_a[:], z2[:], rs_in_col, 1.0, ALU.mult, ALU.mult).then_inc(v_done, 1)

            def finish(b, ff_freed):
                pool.wait_ge(misc_free, ff_freed)
                for t in range(QT):
                    nc.gpsimd.tensor_tensor(f1[:, t, :], f1[:, t, :], fb_rows[:], ALU.add).then_inc(f2_done, 1)
                pool.wait_ge(f2_done, QT * (b + 1))
                nc.gpsimd.tensor_tensor(y[:], y[:], f1[:], ALU.add).then_inc(out_done, 1)

            rstd_of(1, mv_x, var_x, rstd_x, 1)
            split_rows(1, 0)
            split_rows(1, 1)
            pool.wait_ge(consts_done, 1)

            for j, (kind, n) in enumerate(PROLOGUE[2:]):
                split_chunk(kind, n, j + 3, j)

            slot = [0]

            def slot_of(g):
                return slot[0]

            def batch(b, first=False, last=False):
                c = Chunks(b, first, last)

                def split_at(place):
                    if c.at.get(place, ("",))[0] in KV:
                        split_chunk(*c.at[place], c.before(place) + 1, c.before(place, KV))

                for h in range(H):
                    split_at((h - 1, "B"))
                    if not (last and h == H - 1):
                        slot[0] = (h + 1) % 2
                        norm(H * b + h + 1)
                    split_at((h, "A"))
                    if h == 2:
                        if not first:
                            rstd_of(0, mv_y, var_y, rstd_y, b)
                        copy_x(b)
                    if h == 3 and not first:
                        scale_quant_in(b - 1)
                    if h == 7 and not last:
                        rstd_of(1, mv_x, var_x, rstd_x, b + 2)
                    if h == 8 and not first:
                        finish(b - 1, Chunks(b, first, last).through("ff_prev", 0))
                    if h == 10 and not last:
                        pool.wait_ge(misc_full, Chunks(b, first, last).through("v1", 3))
                        split_rows(b + 2, 0)
                    if h == 11 and not last:
                        split_rows(b + 2, 1)

            norm(0)
            batch(0, first=True)
            with pool.Fori(1, B - 1) as b:
                batch(b)
            batch(B - 1, last=True)
            rstd_of(0, mv_y, var_y, rstd_y, B)
            scale_quant_in(B - 1)
            finish(B - 1, TOTAL_CHUNKS)

        @block.tensor
        def _(pe):
            mm = nc.tensor.matmul

            def split_product(dst, a_hi, a_lo, b_hi, b_lo, more=False):
                n = 0
                for t in range(DT):
                    for a, c in ((a_hi, b_hi), (a_lo, b_hi), (a_hi, b_lo)):
                        n += 1
                        last = mm(dst, a(t), c(t), start=(n == 1), stop=(n == 3 * DT and not more))
                return last

            def chunk(c, place, first=False):
                kind, n = c.at[place]
                start = c.before(place)
                pe.wait_ge(misc_free, start)
                if kind == "q":
                    pe.wait_ge(zq_ready, c.before(place, ZQ))
                if kind == "k0" and n == 0:
                    pe.wait_ge(kv_split, 2 * (c.b + 2))
                run_chunk(kind, n, c.b).then_inc(misc_full, 1)

            def run_chunk(kind, n, b):
                if kind == "q":
                    for p in range(GH // 2):
                        cols = slice((n * GH // 2 + p) * P, (n * GH // 2 + p + 1) * P)
                        last = split_product(ps_misc[:, p * S:(p + 1) * S],
                                             lambda t: w_hi["q"][:, t, cols], lambda t: w_lo["q"][:, t, cols],
                                             lambda t: zt_hi[:, t, :], lambda t: zt_lo[:, t, :])
                elif kind in ("k0", "k1"):
                    p = n * GH // 2 + int(kind[1])
                    cols = slice(p * P, (p + 1) * P)
                    for w, keys in (("k", slice(0, S)), ("gk", slice(S, NK))):
                        last = split_product(ps_misc[:, keys],
                                             lambda t: w_hi[w][:, t, cols], lambda t: w_lo[w][:, t, cols],
                                             lambda t: kv_hi[:, t, keys], lambda t: kv_lo[:, t, keys])
                elif kind in ("v0", "v1"):
                    half = int(kind[1])
                    w = ("v", "gv")[half]
                    cols = slice(n * GW, (n + 1) * GW)
                    for i in range(2):
                        keys = slice((2 * half + i) * P, (2 * half + i + 1) * P)
                        dst = ps_misc[:, i * GW:(i + 1) * GW]
                        split_product(dst, lambda t: kv_hi[:, t, keys], lambda t: kv_lo[:, t, keys],
                                      lambda t: w_hi[w][:, t, cols], lambda t: w_lo[w][:, t, cols], more=True)
                        last = mm(dst, vbias_ones[:], vbias[:, half, cols], start=False, stop=True)
                elif kind == "zt_next":
                    pe.wait_ge(z_done, QT * (b + 2))
                    last = transpose_z()
                elif kind == "wo_prev":
                    pe.wait_ge(wo_loaded, 16)
                    pe.wait_ge(o_done, H * b)
                    for t in range(QT):
                        for p in range(H // 2):
                            last = mm(ps_misc[:, t * D:(t + 1) * D], o_t[:, p, t * P:(t + 1) * P], wo_sb[:, p, :],
                                      start=(p == 0), stop=(p == H // 2 - 1))
                elif kind == "xq_prev":
                    pe.wait_ge(xq_done, b)
                    dst = ps_misc[:, 0:256].bitcast(BF16)
                    for t in range(DT):
                        for q in range(QT):
                            last = nc.tensor.transpose(dst[:, t * S + q * P:t * S + (q + 1) * P],
                                                       xq[:, q * D + t * P:q * D + (t + 1) * P], ident_bf[:])
                elif kind == "ff_prev":
                    for q in range(QT):
                        for t in range(DT):
                            last = mm(ps_misc[:, q * D:(q + 1) * D], xq_t[:, t, q * P:(q + 1) * P], ffn_q[:, t, :],
                                      start=(t == 0), stop=(t == DT - 1))
                return last

            def transpose_z():
                for t in range(DT):
                    for q in range(QT):
                        last = nc.tensor.transpose(ps_misc[:, t * S + q * P:t * S + (q + 1) * P],
                                                   scr_a[:, q * D + t * P:q * D + (t + 1) * P], ident[:])
                return last

            def scores(h, g, free=True):
                n, i = h // GH, h % GH
                if free:
                    pe.wait_ge(exp_done, QT * (g - 1))
                for t in range(QT):
                    dst = ps_scores[:, h % 2, t, :]
                    rows = slice(t * P, (t + 1) * P)
                    qh, ql = q_hi[:, n % 2, i, rows], q_lo[:, n % 2, i, rows]
                    kh, kl = k_hi[:, n % 2, i // 2, :], k_lo[:, n % 2, i // 2, :]
                    mm(dst, qh, kh, start=True, stop=False)
                    mm(dst, qh, kl, start=False, stop=False)
                    mm(dst, ql, kh, start=False, stop=False)
                    m = mask_sb[:, n % 2, (i * QT + t) * S:(i * QT + t + 1) * S].bitcast(FP8E5)
                    last = mm(dst[:, 0:S], mask_weight[:], m, start=False, stop=True)
                last.then_inc(scores_done, 1)

            def transposes(h, g, first=False):
                pe.wait_ge(norm_done, QT * (g + 1))
                for k in range(2):
                    if not first:
                        pe.wait_ge(ptlo_done, 2 * g - 1 + k)
                    for j in range(2):
                        for t in range(QT):
                            kt = 2 * k + j
                            last = nc.tensor.transpose(ps_pt[:, k, j, t * P:(t + 1) * P],
                                                       probs[:, h % 2, t, kt * P:(kt + 1) * P], ident[:])
                    last.then_inc(pt_full, 1)

            def outputs(h, g, first=False):
                pe.wait_ge(ptlo_done, 2 * (g + 1))
                if not first:
                    pe.wait_ge(o_done, g)
                n, i = h // GH, h % GH
                for kt in range(KT):
                    for pt in (pt_hi, pt_lo):
                        last = mm(ps_o[:, 0:S], v_hl[:, n % 2, kt, i, :], pt[:, h % 2, kt, :],
                                  start=(kt == 0 and pt is pt_hi), stop=(kt == KT - 1 and pt is pt_lo))
                last.then_inc(o_full, 1)

            pe.wait_ge(consts_done, 1)
            pe.wait_ge(z_done, QT)
            transpose_z().then_inc(misc_full, 1)
            pe.wait_ge(zeros_done, 2)
            for j, (kind, n) in enumerate(PROLOGUE[1:]):
                pe.wait_ge(misc_free, j + 1)
                pe.wait_ge(w_split, {"q": 1, "k0": 3, "k1": 3, "v0": 4, "v1": 5}[kind])
                if kind == "q":
                    pe.wait_ge(zq_ready, 1)
                if kind == "k0":
                    pe.wait_ge(kv_split, 2)
                run_chunk(kind, n, 0).then_inc(misc_full, 1)
            pe.wait_ge(zq_ready, 2)
            pe.wait_ge(kv_ready, 4)
            pe.wait_ge(mask_loaded[0], 16)
            scores(0, 0, free=False)
            scores(1, 1, free=False)

            def batch(b, first=False, last=False):
                c = Chunks(b, first, last)

                def do(place):
                    if place in c.at:
                        chunk(c, place)

                for h in range(H):
                    g = H * b + h
                    ahead = h + 2
                    if not (last and ahead >= H):
                        nxt = ahead // GH % NG
                        if ahead % GH == 0:
                            bb = b + ahead // H
                            pe.wait_ge(mask_loaded[nxt % 2], 16 * (2 * bb + nxt // 2 + 1))
                            pe.wait_ge(zq_ready, c.through("q", nxt, ZQ))
                            pe.wait_ge(kv_ready, c.through("k0", nxt, KV))
                        if ahead % GH == 2:
                            if ahead == 2:
                                if not first:
                                    pe.wait_ge(kv_ready, c.before(FIRST_PLACE, KV))
                            else:
                                pe.wait_ge(kv_ready, c.through("k1", nxt, KV))
                        scores(ahead % H, g + 2)
                    do((h, "A"))
                    transposes(h, g, first and h == 0)
                    if not (first and h == 0):
                        if (h - 1) % GH == 0:
                            n = (h - 1) // GH
                            if n > 0:
                                pe.wait_ge(kv_ready, c.through("v1", n, KV))
                        outputs((h - 1) % H, g - 1, first and h == 1)
                    do((h, "B"))

            batch(0, first=True)
            with pe.Fori(1, B - 1) as b:
                batch(b)
            batch(B - 1, last=True)
            outputs(H - 1, H * B - 1)
            for j, kind in enumerate(PREV):
                pe.wait_ge(misc_free, TAIL_AT + j)
                run_chunk(kind, 0, B).then_inc(misc_full, 1)

        @block.scalar
        def _(act):
            act.wait_ge(zeros_done, 2)

            def copy_out(kind, n):
                if kind in KV:
                    dst = kv_out[:, KV_TURN.get((kind, n)), :]
                else:
                    dst = zq_out[:]
                if kind in ("v0", "v1", "zt_next"):
                    return nc.scalar.copy(dst, ps_misc[:])
                for j in range(2):
                    if kind == "q":
                        bias = qk_bias[:, 0, n * 2 + j:n * 2 + j + 1]
                    else:
                        p = n * 2 + int(kind[1])
                        bias = qk_bias[:, 1 + j, p:p + 1]
                    last = nc.scalar.activation(dst[:, j * S:(j + 1) * S], ps_misc[:, j * S:(j + 1) * S],
                                                ACT.Identity, bias=bias)
                return last

            def chunk(kind, n, before, kv_before, zq_before, b, early=False):
                act.wait_ge(misc_full, before + 1)
                if kind in KV:
                    if not (early and kv_before < 2):
                        act.wait_ge(kv_ready, kv_before - 1)
                    copy_out(kind, n).then_inc(misc_free, 1)
                elif kind in ZQ:
                    if not (early and zq_before < 1):
                        act.wait_ge(zq_ready, zq_before)
                    copy_out(kind, n).then_inc(misc_free, 1)
                elif kind == "xq_prev":
                    nc.scalar.copy(xq_t[:].rearrange("p t s -> p (t s)"),
                                   ps_misc[:, 0:256].bitcast(BF16)).then_inc(misc_free, 1)
                elif kind == "ff_prev":
                    nc.scalar.activation(f1[:].rearrange("p t d -> p (t d)"), ps_misc[:], ACT.Copy,
                                         scale=ss_col).then_inc(misc_free, 1)

            def exps(h, g, free=True):
                act.wait_ge(min_done, g + 1)
                if free:
                    act.wait_ge(pt_full, 2 * (g - 1))
                for t in range(QT):
                    nc.scalar.activation(probs[:, h % 2, t, :], ps_scores[:, h % 2, t, :], ACT.Exp,
                                         bias=neg_max[:, h % 2, t:t + 1], scale=-1.0,
                                         accum_out=sums[:, h % 2, t:t + 1]).then_inc(exp_done, 1)

            def pt_his(h, g, free=True):
                for k in range(2):
                    act.wait_ge(pt_full, 2 * g + k + 1)
                    if free and k == 0:
                        act.wait_ge(o_full, g - 1)
                    nc.scalar.copy(pt_hi[:, h % 2, 2 * k:2 * k + 2, :], ps_pt[:, k, :, :]).then_inc(pthi_done, 1)

            def o_los(g, first=False):
                act.wait_ge(o_full, g + 1)
                if not first:
                    act.wait_ge(o_done, g)
                nc.scalar.copy(o_lo[:], ps_o[DK:P, 0:S]).then_inc(olo_done, 1)

            for j, (kind, n) in enumerate(PROLOGUE):
                if j == 1:
                    act.wait_ge(consts_done, 1)
                kv, zq = (sum(k in kinds for k, _ in PROLOGUE[:j]) for kinds in (KV, ZQ))
                chunk(kind, n, j, kv, zq, 0, early=True)
            exps(0, 0, free=False)

            def batch(b, first=False, last=False):
                c = Chunks(b, first, last)

                def do(place):
                    if place in c.at:
                        chunk(*c.at[place], c.before(place), c.before(place, KV), c.before(place, ZQ), b)

                for h in range(H):
                    g = H * b + h
                    if not (first and h < 2):
                        o_los(g - 2, first and h == 2)
                    if not (last and h == H - 1):
                        exps((h + 1) % H, g + 1, free=not (first and h == 0))
                    do((h, "A"))
                    pt_his(h, g, free=not (first and h < 2))
                    do((h, "B"))

            batch(0, first=True)
            with act.Fori(1, B - 1) as b:
                batch(b)
            batch(B - 1, last=True)
            o_los(H * B - 2)
            o_los(H * B - 1)
            for j, kind in enumerate(PREV):
                if kind != "wo_prev":
                    chunk(kind, 0, TAIL_AT + j, 0, 0, B)

        @block.vector
        def _(dve):
            V = nc.vector

            def e4m3fn(v, t, dst, n, halves=(0, 1)):
                base = QUANT_STEPS * n - QUANT_STEPS

                def step(i, ins):
                    ins.then_inc(quant_chain, 1)
                    dve.wait_ge(quant_chain, base + i)

                if 0 in halves:
                    step(1, V.tensor_scalar(t.bitcast(U32), v.bitcast(U32), 0x7F800000, None, ALU.bitwise_and))
                    step(2, V.tensor_scalar(t, t, E4_MIN_NORMAL, E4_MAGIC, ALU.max, ALU.mult))
                    step(3, V.tensor_tensor(v, v, t, ALU.add))
                if 1 not in halves:
                    return None
                step(4, V.tensor_tensor(v, v, t, ALU.subtract))
                step(5, V.scalar_tensor_tensor(out=t, in0=v, scalar=E4_OVERFLOW, in1=v, op0=ALU.mult, op1=ALU.mult))
                return V.scalar_tensor_tensor(out=dst, in0=t, scalar=0.0, in1=v, op0=ALU.mult, op1=ALU.add)

            def split_chunk(kind, n, copied, before):
                if kind == "q":
                    heads = q_hi[:, n % 2].rearrange("p (a e) s -> p e a s", e=2), \
                        q_lo[:, n % 2].rearrange("p (a e) s -> p e a s", e=2)
                    src = zq_out[:].rearrange("p (a s) -> p a s", s=S)
                    parts = [(heads[0][e * DK:(e + 1) * DK, e], heads[1][e * DK:(e + 1) * DK, e],
                              src[e * DK:(e + 1) * DK]) for e in range(2)]
                else:
                    parts = [(zt_hi[:].rearrange("p t s -> p (t s)"), zt_lo[:].rearrange("p t s -> p (t s)"), zq_out[:])]
                dve.wait_ge(misc_free, copied)
                for hi, _, src in parts:
                    last = V.tensor_copy(hi, src)
                last.then_inc(zq_hi_part, 1)
                dve.wait_ge(zq_hi_part, before + 1)
                for hi, lo, src in parts:
                    last = V.tensor_tensor(lo, src, hi.bitcast(F32), ALU.subtract)
                last.then_inc(zq_ready, 1)

            def moments(which, src, bn_ready, mv_ready, n):
                for t in range(QT):
                    V.bn_stats(stats[:, which, t, :], src[:, t, :]).then_inc(bn_ready, 1)
                for t in range(QT):
                    wait_apart(dve, "dve", bn_ready, QT * (n - 1) + t + 1)
                    V.bn_aggr(mv[:, which, t, :], stats[:, which, t, :]).then_inc(mv_ready, 1)

            def normalise(which, dst, src, done):
                for t in range(QT):
                    V.tensor_scalar(dst[:, t * D:(t + 1) * D], src[:, t, :], mv[:, which, t, 0:1],
                                    rstd[:, which, t:t + 1], ALU.subtract, ALU.mult).then_inc(done, 1)

            def chunk(kind, n, before, zq_before, b):
                if kind in ZQ:
                    split_chunk(kind, n, before + 1, zq_before)
                elif kind == "wo_prev":
                    dve.wait_ge(misc_full, before + 1)
                    dve.wait_ge(xbo_done, b)
                    if not (isinstance(b, int) and b == 1):
                        dve.wait_ge(out_stored, 16 * (b - 1))
                    V.tensor_tensor(y[:].rearrange("p t d -> p (t d)"), ps_misc[:],
                                    xbo[:].rearrange("p t d -> p (t d)"), ALU.add).then_inc(misc_free, 1)
                    dve.wait_ge(misc_free, before + 1)
                    moments(0, y, bn_y, mv_y, b)

            def mins(h, g):
                dve.wait_ge(scores_done, g + 1)
                V.tensor_reduce(neg_max[:, h % 2, :], ps_scores[:, h % 2, :, :], AX_X, ALU.min).then_inc(min_done, 1)

            def recip(h, g):
                dve.wait_ge(exp_done, QT * (g + 1))
                V.reciprocal(recips[:, h % 2, :], sums[:, h % 2, :]).then_inc(recip_done, 1)

            def pt_los(h, g):
                for k in range(2):
                    dve.wait_ge(pthi_done, 2 * g + k + 1)
                    V.tensor_tensor(pt_lo[:, h % 2, 2 * k:2 * k + 2, :], ps_pt[:, k, :, :],
                                    pt_hi[:, h % 2, 2 * k:2 * k + 2, :].bitcast(F32),
                                    ALU.subtract).then_inc(ptlo_done, 1)

            def o_adds(h, g):
                dve.wait_ge(olo_done, g + 1)
                e = h % 2
                V.tensor_tensor(o_t[e * DK:(e + 1) * DK, h // 2, :], ps_o[0:DK, 0:S], o_lo[:],
                                ALU.add).then_inc(o_done, 1)

            dve.wait_ge(x_loaded, 16)
            moments(1, x_sb, bn_x, mv_x, 1)
            V.memzero(q_hi[:].rearrange("p a b c -> p (a b c)").bitcast(F32)).then_inc(zeros_done, 1)
            V.memzero(q_lo[:].rearrange("p a b c -> p (a b c)").bitcast(F32)).then_inc(zeros_done, 1)
            dve.wait_ge(rstd_x, 1)
            normalise(1, scr_a, x_sb, z_done)
            dve.wait_ge(ident_done, 1)
            V.tensor_copy(ident_bf[:], ident[:])
            V.tensor_scalar(mask_weight[:], ident[:], MASK_WEIGHT, None, ALU.mult).then_inc(prep_chain, 1)
            dve.wait_ge(consts_loaded, 16 * 12)
            chain = [1]

            def link(ins):
                chain[0] += 1
                ins.then_inc(prep_chain, 1)
                dve.wait_ge(prep_chain, chain[0])

            link(V.memset(vbias[:], 0.0))
            link(V.memset(vbias_ones[:], 0.0))
            for row in (0, 32, 64):
                link(V.memset(vbias_ones[row:row + 1, :], 1.0))
            link(V.tensor_scalar(qk_bias[:, 0, :], qk_bias[:, 0, :], SCORE_SCALE, None, ALU.mult))
            link(V.reciprocal(scales[:, 2:4], scales[:, 0:2]))
            link(V.tensor_tensor(ss_col, s_in_col, s_k_col, ALU.mult))
            for half in range(2):
                for i, src in enumerate((y, xbo)):
                    row = src[half * 32:half * 32 + 1, :, :].rearrange("p a b -> p (a b)")
                    cols = slice(i * 512, (i + 1) * 512)
                    rest = ps_o[half * 32:half * 32 + 1, :]
                    part = z2[half * 32:half * 32 + 1, :]
                    link(V.tensor_copy(part, row))
                    link(V.tensor_copy(vbias[0:1, half, cols], part))
                    link(V.tensor_tensor(rest, row, part, ALU.subtract))
                    link(V.tensor_copy(part, rest))
                    link(V.tensor_copy(vbias[32:33, half, cols], part))
                    link(V.tensor_tensor(rest, rest, part, ALU.subtract))
                    link(V.tensor_copy(vbias[64:65, half, cols], rest))
            v_w = xbo[:].rearrange("p a b -> p (a b)")
            t_w = y[:].rearrange("p a b -> p (a b)")
            link(V.tensor_scalar(v_w, xq[:], rs_k_col, None, ALU.mult))
            e4m3fn(v_w, t_w, ffn_q[:].rearrange("p t n -> p (t n)"), 1).then_inc(consts_done, 1)

            def split_weight(i):
                n = names[i]
                scale = SCORE_SCALE if n == "q" else 1.0
                raw = stage[i % 2]
                hi = w_hi[n][:].rearrange("p t n -> p (t n)")
                dve.wait_ge(w_loaded[i % 2], 16 * (i // 2 + 1))
                V.tensor_scalar(hi, raw, scale, None, ALU.mult).then_inc(w_hi_done, 1)
                dve.wait_ge(w_hi_done, i + 1)
                V.scalar_tensor_tensor(out=w_lo[n][:].rearrange("p t n -> p (t n)"), in0=raw, scalar=scale,
                                       in1=hi.bitcast(F32), op0=ALU.mult, op1=ALU.subtract).then_inc(w_split, 1)

            split_chunk("zt_next", 0, 1, 0)
            for i in range(len(names)):
                split_weight(i)
            split_chunk("q", 0, 2, 1)
            mins(0, 0)
            mins(1, 1)
            recip(0, 0)

            def quantise(b, half):
                if half == 0:
                    dve.wait_ge(v_done, b)
                last = e4m3fn(scr_a[:], scr_b[:], xq[:], b + 1, (half,))
                if half == 1:
                    last.then_inc(xq_done, 1)

            def normalise_y(b):
                dve.wait_ge(rstd_y, b)
                normalise(0, z2, y, z2_done)

            def batch(b, first=False, last=False):
                c = Chunks(b, first, last)

                def do(place):
                    if place in c.at:
                        chunk(*c.at[place], c.before(place), c.before(place, ZQ), b)

                for h in range(H):
                    g = H * b + h
                    if not (first and h < 2):
                        o_adds((h - 2) % H, g - 2)
                    if not (last and h == H - 1):
                        recip((h + 1) % H, g + 1)
                    if not (last and h >= H - 2):
                        mins((h + 2) % H, g + 2)
                    do((h, "A"))
                    pt_los(h, g)
                    do((h, "B"))
                    if h == 3 and not first:
                        normalise_y(b)
                    if h in (4, 5) and not first:
                        quantise(b, h - 4)
                    if h == 6 and not last:
                        dve.wait_ge(x_loaded, 16 * (b + 2))
                        moments(1, x_sb, bn_x, mv_x, b + 2)
                    if h == 8 and not last:
                        dve.wait_ge(rstd_x, b + 2)
                        normalise(1, scr_a, x_sb, z_done)

            batch(0, first=True)
            with dve.Fori(1, B - 1) as b:
                batch(b)
            batch(B - 1, last=True)
            o_adds(H - 2, H * B - 2)
            o_adds(H - 1, H * B - 1)
            chunk("wo_prev", 0, TAIL_AT, 0, B)
            normalise_y(B)
            quantise(B, 0)
            quantise(B, 1)


def kernel(**inputs):
    import numpy as np
    import concourse.bacc as bacc
    from concourse.bass_utils import run_bass_kernel_spmd

    a = {k: np.asarray(v) for k, v in inputs.items()}
    w = {k[len("L0_xattn_"):]: v for k, v in a.items() if k.startswith("L0_xattn_")}
    m = a["mask_Bx16xSxS_bk1"].reshape(B, H, QT, P, S).transpose(0, 3, 1, 2, 4).reshape(B, P, H * QT * S)

    def columns(name):
        return w[name].reshape(-1, P).T

    arrays = {
        "x": a["x"],
        "side_t": a["fside_BxSxS_0"].transpose(0, 2, 1),
        "ctx_t": a["ctx_1024"].transpose(0, 2, 1),
        "mask": m,
        "wq_t": w["Wq"].T, "bq": columns("bq"), "wk_t": w["Wk"].T, "bk": columns("bk"), "wgk_t": w["Wgk"].T, "bgk": columns("bgk"),
        "wv_t": w["Wv"].T, "bv": w["bv"], "wgv_t": w["Wgv"].T, "bgv": w["bgv"], "wo_t": w["Wo"].T, "bo": w["bo"],
        "ffn_w": a["L0_ffn_kernel"], "s_in": a["L0_ffn_input_scale"], "s_k": a["L0_ffn_kernel_scale"],
        "ffn_bias": a["L0_ffn_bias"],
    }
    arrays = {f"{k}_dram": np.ascontiguousarray(v) for k, v in arrays.items()}
    nc = bacc.Bacc("TRN2", target_bir_lowering=False, num_devices=1,
                   dynamic_dma_scratch_size=4096)
    args = [nc.dram_tensor(k, v.shape, mybir.dt.from_np(v.dtype), kind="ExternalInput").ap()
            for k, v in arrays.items()]
    args.append(nc.dram_tensor("out_dram", (B, S, D), F32, kind="ExternalOutput").ap())
    xattn_ffn_kernel(nc, *args)
    r = run_bass_kernel_spmd(nc, [arrays], core_ids=[0])
    return r.results[0]["out_dram"]
```

```python
from contextlib import ExitStack

import concourse.bass as bass
from concourse import mybir

F32 = mybir.dt.float32
F32R = mybir.dt.float32r
BF16 = mybir.dt.bfloat16
FP8E5 = mybir.dt.float8e5
U8 = mybir.dt.uint8
U32 = mybir.dt.uint32
ALU = mybir.AluOpType
ACT = mybir.ActivationFunctionType
AX_X = mybir.AxisListType.X

P = 128
B, S, D, H = 32, 256, 256, 16
DK = 64
NK = 2 * S
QT = S // P
DT = D // P
KT = NK // P
GH = 4
NG = H // GH
GW = GH * DK
SCORE_SCALE = -1.0 / DK ** 0.5
LN_EPS = 1e-5
MASK_WEIGHT = 2.0 ** 116
E4_MAGIC = 1.5 * 2.0 ** 20
E4_MIN_NORMAL = 2.0 ** -6
E4_OVERFLOW = 1.69e33

PLACES = {
    (0, "A"): ("k0", 1), (0, "B"): ("q", 1), (1, "A"): ("wo0_prev", 0), (1, "B"): ("k1", 1),
    (2, "A"): ("wo1_prev", 0), (2, "B"): ("q", 2), (3, "A"): ("v0", 1), (3, "B"): ("k0", 2), (4, "A"): ("v1", 1),
    (5, "A"): ("v0", 2), (5, "B"): ("k1", 2), (6, "A"): ("v1", 2), (6, "B"): ("q", 3), (7, "A"): ("k0", 3),
    (7, "B"): ("xq_prev", 0), (8, "A"): ("k1", 3), (9, "A"): ("v0", 3), (9, "B"): ("v1", 3),
    (10, "A"): ("zt_next", 0), (10, "B"): ("ff_prev", 0), (11, "B"): ("q", 0),
    (12, "A"): ("k0", 0), (12, "B"): ("v0", 0), (13, "B"): ("k1", 0), (15, "A"): ("v1", 0),
}
B_EARLY = (1, 2)
assert all((h, "B") in PLACES and (h + 1, "A") in PLACES for h in B_EARLY)
LAST_OWN = 10
SLOT_ORDER = [(h, place) for h in range(H) for place in "AB"]
PROLOGUE = [("zt_next", 0), ("q", 0), ("k0", 0), ("v0", 0), ("k1", 0), ("v1", 0)]
WO = ("wo0_prev", "wo1_prev")
PREV = WO + ("xq_prev", "ff_prev")


def chunks_of(first, last):
    def kept(place, chunk):
        kind, group = chunk
        if first and kind in PREV:
            return False
        return not (last and (kind == "zt_next" or place[0] > LAST_OWN))
    return {place: PLACES[place] for place in SLOT_ORDER if place in PLACES and kept(place, PLACES[place])}


FIRST = list(chunks_of(True, False).values())
STEADY = list(chunks_of(False, False).values())
KV = ("k0", "k1", "v0", "v1")
K_KINDS = ("k0", "k1")
V_KINDS = ("v0", "v1")
ZQ = ("zt_next", "q")

assert (H - 1, "B") not in PLACES


def count_before(b, kinds):
    per = sum(kind in kinds for kind, _ in STEADY)
    head = sum(kind in kinds for kind, _ in PROLOGUE)
    if isinstance(b, int) and b == 0:
        return head
    return per * b + (head + sum(kind in kinds for kind, _ in FIRST) - per)


ALL_KINDS = KV + ZQ + PREV
TAIL_AT = count_before(B - 1, ALL_KINDS) + len(chunks_of(False, True))
TOTAL_CHUNKS = TAIL_AT + len(PREV)


KV_TURN = {chunk: i % 2 for i, chunk in enumerate(chunk for chunk in STEADY if chunk[0] in KV)}


class Chunks:

    def __init__(self, b, first=False, last=False):
        self.b, self.at = b, chunks_of(first, last)
        self.order = list(self.at)

    def before(self, place, kinds=ALL_KINDS):
        n = sum(self.at[p][0] in kinds for p in self.order[:self.order.index(place)])
        return count_before(self.b, kinds) + n

    def through(self, kind, group, kinds=ALL_KINDS):
        for p in self.order:
            if self.at[p] == (kind, group):
                return self.before(p, kinds) + 1
        raise KeyError(kind)


def xattn_ffn_kernel(nc, x, side_t, ctx_t, mask, wq_t, bq, wk_t, bk, wgk_t, bgk, wv_t, bv, wgv_t, bgv,
                     wo_t, bo, ffn_w, s_in, s_k, ffn_bias, out):
    with ExitStack() as ctx:
        def sb(name, shape, dt):
            return ctx.enter_context(nc.sbuf_tensor(name, shape, dt))

        def psum(name, shape, dt=F32):
            return ctx.enter_context(nc.psum_tensor(name, shape, dt))

        def sem(name):
            return ctx.enter_context(nc.semaphore(name))

        names = ["q", "k", "gk", "v", "gv"]
        w_hi = {n: sb(f"w{n}_hi", [P, DT, H * DK], F32R) for n in names}
        w_lo = {n: sb(f"w{n}_lo", [P, DT, H * DK], F32R) for n in names}
        wo_sb = sb("wo_sb", [P, H * DK // P, D], F32)
        ffn_q = sb("ffn_q", [P, DT, D], BF16)
        v_bias = sb("v_bias", [P, 2, H * DK], F32)
        qk_bias = sb("qk_bias", [P, 3, H * DK // P], F32)
        bo_rows = sb("bo_rows", [P, D], F32)
        fb_rows = sb("fb_rows", [P, D], BF16)
        scales = sb("scales", [P, 8], F32)
        ident = sb("ident", [P, P], F32)
        ident_bf = sb("ident_bf", [P, P], BF16)
        mask_weight = sb("mask_weight", [P, P], BF16)

        side_raw = sb("side_raw", [P, DT, S], F32)
        kv_hi = sb("kv_hi", [P, DT, NK], F32R)
        kv_lo = sb("kv_lo", [P, DT, NK], F32R)
        x_sb = sb("x_sb", [P, QT, D], F32)
        xbo = sb("xbo", [P, QT, D], F32)
        zt_hi = sb("zt_hi", [P, DT, S], F32R)
        zt_lo = sb("zt_lo", [P, DT, S], F32R)
        o_t = sb("o_t", [P, H // 2, S], F32)
        y = sb("y", [P, QT, D], F32)
        scr_a = sb("scr_a", [P, QT * D], F32)
        scr_b = sb("scr_b", [P, QT * D], F32)
        z2 = sb("z2", [P, QT * D], BF16)
        xq = sb("xq", [P, QT * D], BF16)
        xq_t = z2[:].rearrange("p (t s) -> p t s", t=DT)
        f1 = xq[:].rearrange("p (t d) -> p t d", t=QT)
        stats = sb("stats", [P, 2, QT, 6], F32)
        mv = sb("mv", [P, 2, QT, 2], F32)
        var_eps = sb("var_eps", [P, 2, QT], F32)
        rstd = sb("rstd", [P, 2, QT], F32)
        minus_half = sb("minus_half", [P, QT], F32)

        q_hh = sb("q_hh", [P, 2, GH, S], F32R)
        q_lo = sb("q_lo", [P, 2, GH, S], F32R)
        k_hl = sb("k_hl", [P, 2, GH, NK], F32R)
        v_hl = sb("v_hl", [P, 2, KT, GH, 2 * DK], F32R)
        mask_sb = sb("mask_sb", [P, 2, GH * QT * S], U8)
        k_split = sb("k_split", [P, 2, NK], F32R)
        kv_out = sb("kv_out", [P, 2, 512], F32)
        zq_out = sb("zq_out", [P, 512], F32)
        probs = sb("probs", [P, 2, QT, NK], F32)
        pt_hi = sb("pt_hi", [P, 2, KT, S], F32R)
        pt_lo = sb("pt_lo", [P, 2, KT, S], F32R)
        neg_max = sb("neg_max", [P, 2, QT], F32)
        sums = sb("sums", [P, 2, QT], F32)
        recips = sb("recips", [P, 2, QT], F32)
        o_lo = sb("o_lo", [DK, S], F32)
        o_first = sb("o_first", [DK, S], F32)

        ps_scores = psum("ps_scores", [P, 2, QT, NK])
        ps_pt = psum("ps_pt", [P, 2, 2, S])
        ps_o = psum("ps_o", [P, 512])
        ps_misc = psum("ps_misc", [P, 512])

        w_loaded = {n: sem(f"w_loaded_{n}") for n in names}
        w_split = sem("w_split")
        w_hi_done = sem("w_hi_done")
        consts_loaded = sem("consts_loaded")
        wo_loaded = sem("wo_loaded")
        ident_zero = sem("ident_zero")
        ident_done = sem("ident_done")
        consts_done = sem("consts_done")
        prep_chain = sem("prep_chain")
        zeros_done = sem("zeros_done")
        mask_loaded = [sem("mask_loaded0"), sem("mask_loaded1")]
        side_loaded = sem("side_loaded")
        ctx_loaded = sem("ctx_loaded")
        x_loaded = sem("x_loaded")
        out_stored = sem("out_stored")
        scores_done = sem("scores_done")
        pt_full = sem("pt_full")
        o_full = sem("o_full")
        misc_full = sem("misc_full")
        misc_free = sem("misc_free")
        kv_hi_part = sem("kv_hi_part")
        kv_ready = sem("kv_ready")
        k_placed = sem("k_placed")
        q_placed = sem("q_placed")
        zq_hi_part = sem("zq_hi_part")
        zq_ready = sem("zq_ready")
        exp_done = sem("exp_done")
        pthi_done = sem("pthi_done")
        ptlo_done = sem("ptlo_done")
        olo_done = sem("olo_done")
        o_done = sem("o_done")
        min_done = sem("min_done")
        recip_done = sem("recip_done")
        norm_done = sem("norm_done")
        kvhi_done = sem("kvhi_done")
        kv_split = sem("kv_split")
        xbo_done = sem("xbo_done")
        bn_x = sem("bn_x")
        mv_x = sem("mv_x")
        var_x = sem("var_x")
        rstd_x = sem("rstd_x")
        z_done = sem("z_done")
        bn_y = sem("bn_y")
        mv_y = sem("mv_y")
        var_y = sem("var_y")
        rstd_y = sem("rstd_y")
        z2_done = sem("z2_done")
        v_done = sem("v_done")
        quant_chain = sem("quant_chain")
        xq_done = sem("xq_done")
        f2_done = sem("f2_done")
        out_done = sem("out_done")

        CONSTS = 16 * 10
        W_SCALE = {"q": SCORE_SCALE}
        QUANT_STEPS = 5
        K_PLACES = 16 * 4
        Q_PLACES = 16 * 2
        w_src = {"q": wq_t, "k": wk_t, "gk": wgk_t, "v": wv_t, "gv": wgv_t}
        stages = [probs[:].rearrange("p a b c -> p (a b c)"), o_t[:].rearrange("p a b -> p (a b)"),
                  wo_sb[:].rearrange("p a b -> p (a b)")]
        stage = {n: stages[i % len(stages)] for i, n in enumerate(names)}
        s_in_col, s_k_col, rs_in_col, rs_k_col, ss_col = (scales[:, i:i + 1] for i in range(5))

        def zq_parts(kind, n):
            if kind == "zt_next":
                return [(zt_hi[:].rearrange("p t s -> p (t s)"), zt_lo[:].rearrange("p t s -> p (t s)"), zq_out[:])]
            hh = q_hh[:, n % 2].rearrange("p (a e) s -> p e a s", e=2)
            ql = q_lo[:, n % 2].rearrange("p (a e) s -> p e a s", e=2)
            src = zq_out[:].rearrange("p (a s) -> p a s", s=S)
            owns = [slice(e * DK, (e + 1) * DK) for e in range(2)]
            return [(hh[own, e], ql[own, e], src[own]) for e, own in enumerate(owns)]

        block = ctx.enter_context(nc.Block())

        waits_passed = {e: sem(f"waits_passed_{e}") for e in ("sp", "pool", "dve")}

        def wait_apart(engine, name, semaphore, value):
            engine.wait_ge(semaphore, value)
            engine.sem_inc(waits_passed[name], 1)

        @block.sync
        def _(sp):
            def load_mask(b, n):
                if not (isinstance(b, int) and b == 0 and n < 2):
                    wait_apart(sp, "sp", scores_done, H * b + GH * (n - 1))
                src = one(mask, b).rearrange("o p n -> (o p) n")
                sp.dma_start(mask_sb[:, n % 2, :],
                             src[:, n * GH * QT * S:(n + 1) * GH * QT * S]).then_inc(mask_loaded[n % 2], 16)

            def one(ap, b):
                return ap[b:b + 1] if isinstance(b, int) else ap[bass.ds(b, 1)]

            def load_x(b):
                sp.dma_start(x_sb[:], one(x, b).rearrange("o (t p) d -> p (o t) d", p=P)).then_inc(x_loaded, 16)

            def load_side(b):
                sp.dma_start(side_raw[:],
                             one(side_t, b).rearrange("o (t p) k -> p (o t) k", p=P)).then_inc(side_loaded, 16)

            def load_ctx(b):
                sp.dma_start(scr_b[:].rearrange("p (t k) -> p t k", t=DT),
                             one(ctx_t, b).rearrange("o (t p) k -> p (o t) k", p=P)).then_inc(ctx_loaded, 16)

            def load_weight(n):
                before = names.index(n) - len(stages)
                if before >= 0:
                    sp.wait_ge(w_split, before + 1)
                sp.dma_start(stage[n].rearrange("p (t n) -> p t n", t=DT),
                             w_src[n].rearrange("(t p) n -> p t n", p=P)).then_inc(w_loaded[n], 16)

            def load_const(dst, src):
                sp.dma_start(dst, src).then_inc(consts_loaded, 16)

            def row(src, width):
                return src.rearrange("(o n) -> o n", o=1).broadcast_to([P, width])

            def place_keys(kind, n, kv_through):
                for part, ready in enumerate((kv_hi_part, kv_ready)):
                    wait_apart(sp, "sp", ready, kv_through)
                    for e in range(2):
                        own = slice(e * DK, (e + 1) * DK)
                        to = slice((e ^ part) * DK, ((e ^ part) + 1) * DK)
                        sp.dma_start(k_hl[to, n % 2, 2 * int(kind[1]) + e, :].bitcast(F32),
                                     k_split[own, part, :].bitcast(F32)).then_inc(k_placed, 16)

            def place_queries(n, zq_through):
                wait_apart(sp, "sp", zq_hi_part, zq_through)
                hh = q_hh[:, n % 2].rearrange("p (a e) s -> p e a s", e=2).bitcast(F32)
                for e in range(2):
                    own, other = slice(e * DK, (e + 1) * DK), slice((1 - e) * DK, (2 - e) * DK)
                    sp.dma_start(hh[other, e], hh[own, e]).then_inc(q_placed, 16)

            load_x(0)
            load_weight("q")
            load_side(0)
            load_weight("k")
            load_weight("gk")
            load_ctx(0)
            load_const(qk_bias[:, 0, :], bq)
            load_const(qk_bias[:, 1, :], bk)
            load_const(qk_bias[:, 2, :], bgk)
            load_const(s_in_col, row(s_in, 1))
            load_const(s_k_col, row(s_k, 1))
            load_const(v_bias[:, 0, :], row(bv, H * DK))
            load_const(v_bias[:, 1, :], row(bgv, H * DK))
            load_mask(0, 0)
            load_const(bo_rows[:], row(bo, D))
            load_const(fb_rows[:], row(ffn_bias, D))
            load_const(xq[:].rearrange("p (t n) -> p t n", t=DT), ffn_w.rearrange("(t p) n -> p t n", p=P))
            load_mask(0, 1)
            load_weight("v")
            load_weight("gv")
            sp.wait_ge(w_split, len(stages))
            sp.dma_start(wo_sb[:], wo_t.rearrange("(t p) n -> p t n", p=P)).then_inc(wo_loaded, 16)
            place_queries(0, 2)
            place_keys("k0", 0, 1)
            place_keys("k1", 0, 3)

            def store(b):
                wait_apart(sp, "sp", out_done, b + 1)
                sp.dma_start(one(out, b).rearrange("o (t p) d -> p (o t) d", p=P), y[:]).then_inc(out_stored, 16)

            def batch(b, first=False, last=False):
                c = Chunks(b, first, last)
                for h in range(H):
                    if h == 0:
                        if not first:
                            load_mask(b, 1)
                        if not last:
                            wait_apart(sp, "sp", kv_split, 2 * (b + 1))
                            load_side(b + 1)
                    if h == 2:
                        load_mask(b, 2)
                    if h == 6 and not last:
                        wait_apart(sp, "sp", xbo_done, b + 1)
                        load_x(b + 1)
                    if h == 6:
                        load_mask(b, 3)
                    if h == 8 and not last:
                        if not first:
                            wait_apart(sp, "sp", xq_done, b)
                        load_ctx(b + 1)
                    if h == 10 and not last:
                        load_mask(b + 1, 0)
                    if h == 15 and not first:
                        store(b - 1)
                    for place in ((h, "A"), (h, "B")):
                        kind, n = c.at.get(place, ("", 0))
                        if kind in K_KINDS:
                            place_keys(kind, n, c.before(place, KV) + 1)
                        if kind == "q":
                            place_queries(n, c.before(place, ZQ) + 1)

            batch(0, first=True)
            with sp.Fori(1, B - 1) as b:
                batch(b)
            batch(B - 1, last=True)
            store(B - 1)
            sp.wait_ge(out_stored, 16 * B)

        @block.gpsimd
        def _(pool):
            nc.gpsimd.memset(minus_half[:], -0.5)
            nc.gpsimd.memset(ident[:], 0.0).then_inc(ident_zero, 1)
            pool.wait_ge(ident_zero, 1)
            nc.gpsimd.affine_select(out=ident[:], in_=ident[:], compare_op=ALU.not_equal, fill=1.0, base=0,
                                    pattern=[[-1, P]], channel_multiplier=1).then_inc(ident_done, 1)

            def rstd_of(which, mv_ready, var_ready, rstd_ready, n):
                wait_apart(pool, "pool", mv_ready, QT * n)
                nc.gpsimd.tensor_scalar(var_eps[:, which, :], mv[:, which, :, 1], 1.0, LN_EPS,
                                        ALU.mult, ALU.add).then_inc(var_ready, 1)
                pool.wait_ge(var_ready, n)
                nc.gpsimd.tensor_tensor(rstd[:, which, :], var_eps[:, which, :], minus_half[:],
                                        ALU.pow).then_inc(rstd_ready, 1)

            def split_rows(n, part):
                loaded = (side_loaded, ctx_loaded)[part]
                raw = (side_raw[:], scr_b[:].rearrange("p (t k) -> p t k", t=DT))[part]
                keys = slice(part * S, (part + 1) * S)
                wait_apart(pool, "pool", loaded, 16 * n)
                nc.gpsimd.tensor_scalar(kv_hi[:, :, keys], raw, 1.0, 0.0, ALU.mult, ALU.add).then_inc(kvhi_done, 1)
                pool.wait_ge(kvhi_done, 2 * (n - 1) + part + 1)
                nc.gpsimd.tensor_tensor(kv_lo[:, :, keys], raw, kv_hi[:, :, keys].bitcast(F32),
                                        ALU.subtract).then_inc(kv_split, 1)

            def copy_x(b):
                pool.wait_ge(z_done, QT * (b + 1))
                for t in range(QT):
                    i = nc.gpsimd.tensor_tensor(xbo[:, t, :], x_sb[:, t, :], bo_rows[:], ALU.add)
                i.then_inc(xbo_done, 1)

            def split_chunk(kind, n, copied, before, k_before):
                src = kv_out[:, KV_TURN[kind, n], :]
                r = n % 2
                if kind in K_KINDS:
                    hi, lo = k_split[:, 0, :], k_split[:, 1, :]
                else:
                    half = int(kind[1])
                    v = v_hl[:, r, 2 * half:2 * half + 2, :, :].rearrange("p k h d -> p (k h) d")
                    src = src.rearrange("p (k d) -> p k d", d=DK)
                    hi, lo = v[:, :, 0:DK], v[:, :, DK:2 * DK]
                wait_apart(pool, "pool", misc_free, copied)
                if kind in K_KINDS and not (isinstance(k_before, int) and k_before == 0):
                    wait_apart(pool, "pool", k_placed, K_PLACES * k_before)
                nc.gpsimd.tensor_scalar(hi, src, 1.0, 0.0, ALU.mult, ALU.add).then_inc(kv_hi_part, 1)
                pool.wait_ge(kv_hi_part, before + 1)
                nc.gpsimd.tensor_tensor(lo, src, hi.bitcast(F32), ALU.subtract).then_inc(kv_ready, 1)

            def norm(h, g):
                wait_apart(pool, "pool", recip_done, g + 1)
                for t in range(QT):
                    nc.gpsimd.tensor_scalar(probs[:, h % 2, t, :], probs[:, h % 2, t, :],
                                            recips[:, h % 2, t:t + 1], 1.0,
                                            ALU.mult, ALU.mult).then_inc(norm_done, 1)

            def scale_quant_in(b):
                wait_apart(pool, "pool", z2_done, QT * (b + 1))
                nc.gpsimd.tensor_scalar(scr_a[:], z2[:], rs_in_col, 1.0, ALU.mult, ALU.mult).then_inc(v_done, 1)

            def finish(b, ff_freed):
                pool.wait_ge(misc_free, ff_freed)
                for t in range(QT):
                    nc.gpsimd.tensor_tensor(f1[:, t, :], f1[:, t, :], fb_rows[:], ALU.add).then_inc(f2_done, 1)
                pool.wait_ge(f2_done, QT * (b + 1))
                nc.gpsimd.tensor_tensor(y[:], y[:], f1[:], ALU.add).then_inc(out_done, 1)

            rstd_of(1, mv_x, var_x, rstd_x, 1)
            nc.gpsimd.memset(q_lo[:].rearrange("p a b c -> p (a b c)").bitcast(F32), 0.0).then_inc(zeros_done, 1)
            split_rows(1, 0)
            split_rows(1, 1)
            pool.wait_ge(consts_done, 1)

            for j, (kind, n) in enumerate(PROLOGUE[2:]):
                split_chunk(kind, n, j + 3, j, sum(k in K_KINDS for k, _ in PROLOGUE[2:2 + j]))

            def batch(b, first=False, last=False):
                c = Chunks(b, first, last)

                def split_at(place):
                    if c.at.get(place, ("",))[0] in KV:
                        split_chunk(*c.at[place], c.before(place) + 1, c.before(place, KV), c.before(place, K_KINDS))

                for h in range(H):
                    split_at((h - 1, "B"))
                    if h == 11 and not last:
                        pool.wait_ge(misc_full, c.through("v1", 3))
                        split_rows(b + 2, 1)
                    if not (last and h == H - 1):
                        norm(h + 1, H * b + h + 1)
                    if h == 3 and not first:
                        rstd_of(0, mv_y, var_y, rstd_y, b)
                    split_at((h, "A"))
                    if h == 5:
                        copy_x(b)
                    if h == 4 and not first:
                        scale_quant_in(b - 1)
                    if h == 8 and not last:
                        rstd_of(1, mv_x, var_x, rstd_x, b + 2)
                    if h == 14 and not first:
                        finish(b - 1, Chunks(b, first, last).through("ff_prev", 0))
                    if h == 10 and not last:
                        pool.wait_ge(misc_full, c.through("v0", 3))
                        split_rows(b + 2, 0)

            norm(0, 0)
            batch(0, first=True)
            with pool.Fori(1, B - 1) as b:
                batch(b)
            batch(B - 1, last=True)
            rstd_of(0, mv_y, var_y, rstd_y, B)
            scale_quant_in(B - 1)
            finish(B - 1, TOTAL_CHUNKS)

        @block.tensor
        def _(pe):
            mm = nc.tensor.matmul

            def split_product(dst, a_hi, a_lo, b_hi, b_lo):
                n = 0
                for t in range(DT):
                    for a, c in ((a_hi, b_hi), (a_lo, b_hi), (a_hi, b_lo)):
                        n += 1
                        last = mm(dst, a(t), c(t), start=(n == 1), stop=(n == 3 * DT))
                return last

            def chunk(c, place, first=False):
                kind, n = c.at[place]
                start = c.before(place)
                pe.wait_ge(misc_free, start)
                if kind == "q" and n == 0:
                    pe.wait_ge(zq_ready, c.before(place, ZQ))
                if kind == "k0" and n == 0:
                    pe.wait_ge(kv_split, 2 * (c.b + 2))
                run_chunk(kind, n, c.b).then_inc(misc_full, 1)

            def run_chunk(kind, n, b):
                if kind == "q":
                    for p in range(GH // 2):
                        cols = slice((n * GH // 2 + p) * P, (n * GH // 2 + p + 1) * P)
                        last = split_product(ps_misc[:, p * S:(p + 1) * S],
                                             lambda t: w_hi["q"][:, t, cols], lambda t: w_lo["q"][:, t, cols],
                                             lambda t: zt_hi[:, t, :], lambda t: zt_lo[:, t, :])
                elif kind in ("k0", "k1"):
                    p = n * GH // 2 + int(kind[1])
                    cols = slice(p * P, (p + 1) * P)
                    for w, keys in (("k", slice(0, S)), ("gk", slice(S, NK))):
                        last = split_product(ps_misc[:, keys],
                                             lambda t: w_hi[w][:, t, cols], lambda t: w_lo[w][:, t, cols],
                                             lambda t: kv_hi[:, t, keys], lambda t: kv_lo[:, t, keys])
                elif kind in ("v0", "v1"):
                    half = int(kind[1])
                    w = ("v", "gv")[half]
                    cols = slice(n * GW, (n + 1) * GW)
                    for i in range(2):
                        keys = slice((2 * half + i) * P, (2 * half + i + 1) * P)
                        dst = ps_misc[:, i * GW:(i + 1) * GW]
                        last = split_product(dst, lambda t: kv_hi[:, t, keys], lambda t: kv_lo[:, t, keys],
                                             lambda t: w_hi[w][:, t, cols], lambda t: w_lo[w][:, t, cols])
                elif kind == "zt_next":
                    pe.wait_ge(z_done, QT * (b + 2))
                    last = transpose_z()
                elif kind in WO:
                    pe.wait_ge(wo_loaded, 16)
                    pe.wait_ge(o_done, H * b)
                    t = WO.index(kind)
                    for p in range(H // 2):
                        last = mm(ps_misc[:, t * D:(t + 1) * D], o_t[:, p, t * P:(t + 1) * P], wo_sb[:, p, :],
                                  start=(p == 0), stop=(p == H // 2 - 1))
                elif kind == "xq_prev":
                    pe.wait_ge(xq_done, b)
                    dst = ps_misc[:, 0:256].bitcast(BF16)
                    for t in range(DT):
                        for q in range(QT):
                            last = nc.tensor.transpose(dst[:, t * S + q * P:t * S + (q + 1) * P],
                                                       xq[:, q * D + t * P:q * D + (t + 1) * P], ident_bf[:])
                elif kind == "ff_prev":
                    for q in range(QT):
                        for t in range(DT):
                            last = mm(ps_misc[:, q * D:(q + 1) * D], xq_t[:, t, q * P:(q + 1) * P], ffn_q[:, t, :],
                                      start=(t == 0), stop=(t == DT - 1))
                return last

            def transpose_z():
                for t in range(DT):
                    for q in range(QT):
                        last = nc.tensor.transpose(ps_misc[:, t * S + q * P:t * S + (q + 1) * P],
                                                   scr_a[:, q * D + t * P:q * D + (t + 1) * P], ident[:])
                return last

            def scores(h, g, free=True):
                n, i = h // GH, h % GH
                if free:
                    pe.wait_ge(exp_done, QT * (g - 1))
                for t in range(QT):
                    dst = ps_scores[:, h % 2, t, :]
                    rows = slice(t * P, (t + 1) * P)
                    mm(dst, q_hh[:, n % 2, i, rows], k_hl[:, n % 2, i, :], start=True, stop=False)
                    mm(dst, q_lo[:, n % 2, i, rows], k_hl[:, n % 2, i, :], start=False, stop=False)
                    m = mask_sb[:, n % 2, (i * QT + t) * S:(i * QT + t + 1) * S].bitcast(FP8E5)
                    last = mm(dst[:, 0:S], mask_weight[:], m, start=False, stop=True)
                last.then_inc(scores_done, 1)

            def transposes(h, g, first=False):
                pe.wait_ge(norm_done, QT * (g + 1))
                for k in range(2):
                    if not first:
                        pe.wait_ge(ptlo_done, 2 * g - 1 + k)
                    for j in range(2):
                        for t in range(QT):
                            kt = 2 * k + j
                            last = nc.tensor.transpose(ps_pt[:, k, j, t * P:(t + 1) * P],
                                                       probs[:, h % 2, t, kt * P:(kt + 1) * P], ident[:])
                    last.then_inc(pt_full, 1)

            def outputs(h, g, first=False, tiles=range(KT)):
                if 0 in tiles:
                    pe.wait_ge(ptlo_done, 2 * (g + 1))
                    if not first:
                        pe.wait_ge(o_done, g)
                n, i = h // GH, h % GH
                for kt in tiles:
                    for pt in (pt_hi, pt_lo):
                        last = mm(ps_o[:, 0:S], v_hl[:, n % 2, kt, i, :], pt[:, h % 2, kt, :],
                                  start=(kt == 0 and pt is pt_hi), stop=(kt == KT - 1 and pt is pt_lo))
                if KT - 1 in tiles:
                    last.then_inc(o_full, 1)

            pe.wait_ge(ident_done, 1)
            pe.wait_ge(z_done, QT)
            transpose_z().then_inc(misc_full, 1)
            for j, (kind, n) in enumerate(PROLOGUE[1:]):
                pe.wait_ge(misc_free, j + 1)
                pe.wait_ge(w_split, {"q": 1, "k0": 3, "k1": 3, "v0": 4, "v1": 5}[kind])
                if kind == "q":
                    pe.wait_ge(zq_ready, 1)
                if kind == "k0":
                    pe.wait_ge(kv_split, 2)
                run_chunk(kind, n, 0).then_inc(misc_full, 1)
            pe.wait_ge(zq_ready, 2)
            pe.wait_ge(kv_ready, 4)
            pe.wait_ge(k_placed, K_PLACES * 2)
            pe.wait_ge(q_placed, Q_PLACES)
            pe.wait_ge(mask_loaded[0], 16)
            pe.wait_ge(consts_done, 1)
            scores(0, 0, free=False)
            scores(1, 1, free=False)

            def batch(b, first=False, last=False):
                c = Chunks(b, first, last)

                def do(place):
                    if place in c.at:
                        chunk(c, place)

                for h in range(H):
                    g = H * b + h
                    ahead = h + 2
                    if not (last and ahead >= H):
                        nxt = ahead // GH % NG
                        if ahead % GH == 0:
                            bb = b + ahead // H
                            pe.wait_ge(mask_loaded[nxt % 2], 16 * (2 * bb + nxt // 2 + 1))
                            pe.wait_ge(zq_ready, c.through("q", nxt, ZQ))
                            pe.wait_ge(q_placed, Q_PLACES * c.through("q", nxt, ("q",)))
                            pe.wait_ge(k_placed, K_PLACES * c.through("k0", nxt, K_KINDS))
                        if ahead % GH == 2:
                            if ahead == 2:
                                if not first:
                                    pe.wait_ge(k_placed, K_PLACES * count_before(b, K_KINDS))
                            else:
                                pe.wait_ge(k_placed, K_PLACES * c.through("k1", nxt, K_KINDS))
                        scores(ahead % H, g + 2)
                    do((h, "A"))
                    transposes(h, g, first and h == 0)
                    if not (first and h == 0):
                        if (h - 1) % GH == 0:
                            n = (h - 1) // GH
                            if n > 0:
                                pe.wait_ge(kv_ready, c.through("v1", n, KV))
                        outputs((h - 1) % H, g - 1, first and h == 1, range(KT - 1))
                    if h in B_EARLY:
                        do((h, "B"))
                    if not (first and h == 0):
                        outputs((h - 1) % H, g - 1, tiles=[KT - 1])
                    if h not in B_EARLY:
                        do((h, "B"))

            batch(0, first=True)
            with pe.Fori(1, B - 1) as b:
                batch(b)
            batch(B - 1, last=True)
            outputs(H - 1, H * B - 1)
            for j, kind in enumerate(PREV):
                pe.wait_ge(misc_free, TAIL_AT + j)
                run_chunk(kind, 0, B).then_inc(misc_full, 1)

        @block.scalar
        def _(act):
            def copy_out(kind, n):
                if kind in KV:
                    dst = kv_out[:, KV_TURN.get((kind, n)), :]
                else:
                    dst = zq_out[:]
                if kind == "zt_next":
                    return nc.scalar.copy(dst, ps_misc[:])
                for j in range(2):
                    if kind == "q":
                        bias = qk_bias[:, 0, n * 2 + j:n * 2 + j + 1]
                    else:
                        p = n * 2 + int(kind[1])
                        bias = qk_bias[:, 1 + j, p:p + 1]
                    last = nc.scalar.activation(dst[:, j * S:(j + 1) * S], ps_misc[:, j * S:(j + 1) * S],
                                                ACT.Identity, bias=bias)
                return last

            def chunk(kind, n, before, kv_before, zq_before, b, early=False):
                if kind in V_KINDS:
                    return
                act.wait_ge(misc_full, before + 1)
                if kind in KV:
                    if not (early and kv_before < 2):
                        act.wait_ge(kv_ready, kv_before - 1)
                    copy_out(kind, n).then_inc(misc_free, 1)
                elif kind in ZQ:
                    if not (early and zq_before < 1):
                        act.wait_ge(zq_ready, zq_before)
                    copy_out(kind, n).then_inc(misc_free, 1)
                elif kind == "xq_prev":
                    nc.scalar.copy(xq_t[:].rearrange("p t s -> p (t s)"),
                                   ps_misc[:, 0:256].bitcast(BF16)).then_inc(misc_free, 1)
                elif kind == "ff_prev":
                    nc.scalar.activation(f1[:].rearrange("p t d -> p (t d)"), ps_misc[:], ACT.Copy,
                                         scale=ss_col).then_inc(misc_free, 1)

            def zq_his(kind, n, before):
                act.wait_ge(misc_free, before + 1)
                for hi, _, src in zq_parts(kind, n):
                    last = nc.scalar.copy(hi, src)
                last.then_inc(zq_hi_part, 1)

            def exps(h, g, free=True):
                act.wait_ge(min_done, g + 1)
                if free:
                    act.wait_ge(pt_full, 2 * (g - 1))
                for t in range(QT):
                    nc.scalar.activation(probs[:, h % 2, t, :], ps_scores[:, h % 2, t, :], ACT.Exp,
                                         bias=neg_max[:, h % 2, t:t + 1], scale=-1.0,
                                         accum_out=sums[:, h % 2, t:t + 1]).then_inc(exp_done, 1)

            def pt_his(h, g, free=True):
                for k in range(2):
                    act.wait_ge(pt_full, 2 * g + k + 1)
                    if free and k == 0:
                        act.wait_ge(o_full, g - 1)
                    nc.scalar.copy(pt_hi[:, h % 2, 2 * k:2 * k + 2, :], ps_pt[:, k, :, :]).then_inc(pthi_done, 1)

            def o_los(g, first=False):
                act.wait_ge(o_full, g + 1)
                if not first:
                    act.wait_ge(o_done, g)
                nc.scalar.copy(o_lo[:], ps_o[DK:P, 0:S]).then_inc(olo_done, 1)

            def weight_hi(n):
                act.wait_ge(w_loaded[n], 16)
                nc.scalar.activation(w_hi[n][:].rearrange("p t n -> p (t n)"), stage[n], ACT.Copy,
                                     scale=W_SCALE.get(n, 1.0)).then_inc(w_hi_done, 1)

            hi_after = {"q": ("v",), "k0": ("gv",)}
            weight_hi("q")
            for j, (kind, n) in enumerate(PROLOGUE):
                if j == 1:
                    weight_hi("k")
                    weight_hi("gk")
                    act.wait_ge(consts_done, 1)
                kv, zq = (sum(k in kinds for k, _ in PROLOGUE[:j]) for kinds in (KV, ZQ))
                chunk(kind, n, j, kv, zq, 0, early=True)
                if kind in ZQ:
                    zq_his(kind, n, j)
                for w in hi_after.get(kind, ()):
                    weight_hi(w)
            exps(0, 0, free=False)

            def batch(b, first=False, last=False):
                c = Chunks(b, first, last)

                def do(place):
                    if place in c.at:
                        chunk(*c.at[place], c.before(place), c.before(place, KV), c.before(place, ZQ), b)

                def his_of(place):
                    if c.at.get(place, ("",))[0] in ZQ:
                        zq_his(*c.at[place], c.before(place))

                for h in range(H):
                    g = H * b + h
                    if not (last and h == H - 1):
                        exps((h + 1) % H, g + 1, free=not (first and h == 0))
                    his_of((h - 1, "B"))
                    do((h, "A"))
                    pt_his(h, g, free=not (first and h < 2))
                    if h in B_EARLY:
                        do((h, "B"))
                    if not (first and h == 0):
                        o_los(g - 1, first and h == 1)
                    if h not in B_EARLY:
                        do((h, "B"))
                    his_of((h, "A"))

            batch(0, first=True)
            with act.Fori(1, B - 1) as b:
                batch(b)
            batch(B - 1, last=True)
            o_los(H * B - 1)
            for j, kind in enumerate(PREV):
                if kind not in WO:
                    chunk(kind, 0, TAIL_AT + j, 0, 0, B)

        @block.vector
        def _(dve):
            V = nc.vector

            def e4m3fn(v, t, dst, n, halves=(0, 1)):
                base = QUANT_STEPS * n - QUANT_STEPS

                def step(i, ins):
                    ins.then_inc(quant_chain, 1)
                    dve.wait_ge(quant_chain, base + i)

                if 0 in halves:
                    step(1, V.tensor_scalar(t.bitcast(U32), v.bitcast(U32), 0x7F800000, None, ALU.bitwise_and))
                    step(2, V.tensor_scalar(t, t, E4_MIN_NORMAL, E4_MAGIC, ALU.max, ALU.mult))
                    step(3, V.tensor_tensor(v, v, t, ALU.add))
                if 1 not in halves:
                    return None
                step(4, V.tensor_tensor(v, v, t, ALU.subtract))
                step(5, V.scalar_tensor_tensor(out=t, in0=v, scalar=E4_OVERFLOW, in1=v, op0=ALU.mult, op1=ALU.mult))
                return V.scalar_tensor_tensor(out=dst, in0=t, scalar=0.0, in1=v, op0=ALU.mult, op1=ALU.add)

            def zq_los(kind, n, before):
                dve.wait_ge(zq_hi_part, before + 1)
                for hi, lo, src in zq_parts(kind, n):
                    last = V.tensor_tensor(lo, src, hi.bitcast(F32), ALU.subtract)
                last.then_inc(zq_ready, 1)

            def moments(which, src, bn_ready, mv_ready, n):
                for t in range(QT):
                    V.bn_stats(stats[:, which, t, :], src[:, t, :]).then_inc(bn_ready, 1)
                for t in range(QT):
                    wait_apart(dve, "dve", bn_ready, QT * (n - 1) + t + 1)
                    V.bn_aggr(mv[:, which, t, :], stats[:, which, t, :]).then_inc(mv_ready, 1)

            def normalise(which, dst, src, done):
                for t in range(QT):
                    V.tensor_scalar(dst[:, t * D:(t + 1) * D], src[:, t, :], mv[:, which, t, 0:1],
                                    rstd[:, which, t:t + 1], ALU.subtract, ALU.mult).then_inc(done, 1)

            def copy_values(kind, n, before, kv_before, kv_wait=True):
                cols = slice(n * GW, (n + 1) * GW)
                dve.wait_ge(misc_full, before + 1)
                if kv_wait:
                    dve.wait_ge(kv_ready, kv_before - 1)
                bias = v_bias[:, int(kind[1]):int(kind[1]) + 1, cols].broadcast_to([P, 2, GW])
                V.tensor_tensor(kv_out[:, KV_TURN[kind, n], :].rearrange("p (k c) -> p k c", c=GW),
                                ps_misc[:].rearrange("p (k c) -> p k c", c=GW), bias, ALU.add).then_inc(misc_free, 1)

            def chunk(kind, n, before, kv_before, b):
                if kind in V_KINDS:
                    copy_values(kind, n, before, kv_before)
                elif kind in WO:
                    t = WO.index(kind)
                    dve.wait_ge(misc_full, before + 1)
                    dve.wait_ge(xbo_done, b)
                    if t == 0 and not (isinstance(b, int) and b == 1):
                        dve.wait_ge(out_stored, 16 * (b - 1))
                    V.tensor_tensor(y[:, t, :], ps_misc[:, t * D:(t + 1) * D], xbo[:, t, :],
                                    ALU.add).then_inc(misc_free, 1)
                    if t == QT - 1:
                        dve.wait_ge(misc_free, before + 1)
                        moments(0, y, bn_y, mv_y, b)

            def mins(h, g):
                dve.wait_ge(scores_done, g + 1)
                V.tensor_reduce(neg_max[:, h % 2, :], ps_scores[:, h % 2, :, :], AX_X, ALU.min).then_inc(min_done, 1)

            def recip(h, g):
                dve.wait_ge(exp_done, QT * (g + 1))
                V.reciprocal(recips[:, h % 2, :], sums[:, h % 2, :]).then_inc(recip_done, 1)

            def pt_los(h, g):
                for k in range(2):
                    dve.wait_ge(pthi_done, 2 * g + k + 1)
                    V.tensor_tensor(pt_lo[:, h % 2, 2 * k:2 * k + 2, :], ps_pt[:, k, :, :],
                                    pt_hi[:, h % 2, 2 * k:2 * k + 2, :].bitcast(F32),
                                    ALU.subtract).then_inc(ptlo_done, 1)

            def o_adds(h, g):
                dve.wait_ge(olo_done, g + 1)
                e = h % 2
                dst = o_first[:] if h == 0 else o_t[e * DK:(e + 1) * DK, h // 2, :]
                V.tensor_tensor(dst, ps_o[0:DK, 0:S], o_lo[:],
                                ALU.add).then_inc(o_done, 1)

            dve.wait_ge(x_loaded, 16)
            moments(1, x_sb, bn_x, mv_x, 1)
            dve.wait_ge(ident_done, 1)
            V.tensor_copy(ident_bf[:], ident[:])
            V.tensor_scalar(mask_weight[:], ident[:], MASK_WEIGHT, None, ALU.mult)
            dve.wait_ge(rstd_x, 1)
            normalise(1, scr_a, x_sb, z_done)

            def weight_lo(i):
                n = names[i]
                hi = w_hi[n][:].rearrange("p t n -> p (t n)")
                dve.wait_ge(w_hi_done, i + 1)
                V.scalar_tensor_tensor(out=w_lo[n][:].rearrange("p t n -> p (t n)"), in0=stage[n],
                                       scalar=W_SCALE.get(n, 1.0), in1=hi.bitcast(F32),
                                       op0=ALU.mult, op1=ALU.subtract).then_inc(w_split, 1)

            weight_lo(0)
            zq_los("zt_next", 0, 0)
            weight_lo(1)
            weight_lo(2)
            dve.wait_ge(consts_loaded, CONSTS)
            V.tensor_scalar(qk_bias[:, 0, :], qk_bias[:, 0, :], SCORE_SCALE, None, ALU.mult)
            V.reciprocal(scales[:, 2:4], scales[:, 0:2])
            V.tensor_tensor(ss_col, s_in_col, s_k_col, ALU.mult).then_inc(consts_done, 1)
            dve.wait_ge(zeros_done, 1)
            zq_los("q", 0, 1)
            weight_lo(3)
            copy_values("v0", 0, 3, 1, kv_wait=False)
            weight_lo(4)
            copy_values("v1", 0, 5, 3)
            mins(0, 0)
            mins(1, 1)
            recip(0, 0)

            def quantise_weights(half):
                v_w, t_w = scr_a[:], y[:].rearrange("p a b -> p (a b)")
                if half == 0:
                    dve.wait_ge(consts_done, 1)
                    V.tensor_scalar(v_w, xq[:], rs_k_col, None, ALU.mult).then_inc(prep_chain, 1)
                    dve.wait_ge(prep_chain, 1)
                e4m3fn(v_w, t_w, ffn_q[:].rearrange("p t n -> p (t n)"), 1, (half,))

            def quantise(b, half):
                if half == 0:
                    dve.wait_ge(v_done, b)
                last = e4m3fn(scr_a[:], scr_b[:], xq[:], b + 1, (half,))
                if half == 1:
                    last.then_inc(xq_done, 1)

            def normalise_y(b):
                dve.wait_ge(rstd_y, b)
                normalise(0, z2, y, z2_done)

            def batch(b, first=False, last=False):
                c = Chunks(b, first, last)

                def do(place):
                    if place in c.at:
                        chunk(*c.at[place], c.before(place), c.before(place, KV), b)

                def los_of(place):
                    if c.at.get(place, ("",))[0] in ZQ:
                        zq_los(*c.at[place], c.before(place, ZQ))

                for h in range(H):
                    g = H * b + h
                    if not (last and h == H - 1):
                        recip((h + 1) % H, g + 1)
                    if not (last and h >= H - 2):
                        mins((h + 2) % H, g + 2)
                    do((h, "A"))
                    los_of((h - 1, "B"))
                    if h == 9 and not last:
                        dve.wait_ge(rstd_x, b + 2)
                        normalise(1, scr_a, x_sb, z_done)
                    if h == 3:
                        dve.wait_ge(o_done, g - 2)
                        V.tensor_copy(o_t[0:DK, 0, :], o_first[:])
                    pt_los(h, g)
                    if h in B_EARLY:
                        do((h, "B"))
                    if not (first and h == 0):
                        o_adds((h - 1) % H, g - 1)
                    if h not in B_EARLY:
                        do((h, "B"))
                    los_of((h, "A"))
                    if h == 3 and not first:
                        normalise_y(b)
                    if h in (4, 5) and first:
                        quantise_weights(h - 4)
                    if h in (5, 6) and not first:
                        quantise(b, h - 5)
                    if h == 7 and not last:
                        dve.wait_ge(x_loaded, 16 * (b + 2))
                        moments(1, x_sb, bn_x, mv_x, b + 2)

            batch(0, first=True)
            with dve.Fori(1, B - 1) as b:
                batch(b)
            batch(B - 1, last=True)
            o_adds(H - 1, H * B - 1)
            for t, kind in enumerate(WO):
                chunk(kind, 0, TAIL_AT + t, 0, B)
            normalise_y(B)
            quantise(B, 0)
            quantise(B, 1)


def kernel(**inputs):
    import numpy as np
    import concourse.bacc as bacc
    from concourse.bass_utils import run_bass_kernel_spmd

    a = {k: np.asarray(v) for k, v in inputs.items()}
    w = {k[len("L0_xattn_"):]: v for k, v in a.items() if k.startswith("L0_xattn_")}
    m = a["mask_Bx16xSxS_bk1"].reshape(B, H, QT, P, S).transpose(0, 3, 1, 2, 4).reshape(B, P, H * QT * S)

    def columns(name):
        return w[name].reshape(-1, P).T

    arrays = {
        "x": a["x"],
        "side_t": a["fside_BxSxS_0"].transpose(0, 2, 1),
        "ctx_t": a["ctx_1024"].transpose(0, 2, 1),
        "mask": m,
        "wq_t": w["Wq"].T, "bq": columns("bq"), "wk_t": w["Wk"].T, "bk": columns("bk"), "wgk_t": w["Wgk"].T, "bgk": columns("bgk"),
        "wv_t": w["Wv"].T, "bv": w["bv"], "wgv_t": w["Wgv"].T, "bgv": w["bgv"], "wo_t": w["Wo"].T, "bo": w["bo"],
        "ffn_w": a["L0_ffn_kernel"], "s_in": a["L0_ffn_input_scale"], "s_k": a["L0_ffn_kernel_scale"],
        "ffn_bias": a["L0_ffn_bias"],
    }
    arrays = {f"{k}_dram": np.ascontiguousarray(v) for k, v in arrays.items()}
    nc = bacc.Bacc("TRN2", target_bir_lowering=False, num_devices=1,
                   dynamic_dma_scratch_size=1024)
    args = [nc.dram_tensor(k, v.shape, mybir.dt.from_np(v.dtype), kind="ExternalInput").ap()
            for k, v in arrays.items()]
    args.append(nc.dram_tensor("out_dram", (B, S, D), F32, kind="ExternalOutput").ap())
    xattn_ffn_kernel(nc, *args)
    r = run_bass_kernel_spmd(nc, [arrays], core_ids=[0])
    return r.results[0]["out_dram"]
```
